# Optimizing a Trainium2 kernel written in Bass

```python
import numpy as np
import jax
import jax.numpy as jnp

def _softmax(x, axis=-1):
    return jax.nn.softmax(x, axis=axis)

def _gelu(x):
    return jax.nn.gelu(x, approximate=True)

def _silu(x):
    return jax.nn.silu(x)

def _sigmoid(x):
    return jax.nn.sigmoid(x)

def _layernorm(x, axis=-1, eps=1e-05):
    m = jnp.mean(x, axis=axis, keepdims=True)
    v = jnp.var(x, axis=axis, keepdims=True)
    return (x - m) / jnp.sqrt(v + eps)

def _scatter_add(tgt, idx, src, axis=0):
    return tgt.at[idx].add(src)

def _segment_sum(src, seg, n):
    return jax.ops.segment_sum(src, seg, n)
kernel_name = 'mk_seq_preln_d1_jaxref_r2_0fa339'

def setup_inputs(seed: int=0):
    np.random.seed(seed)
    _w = jnp.asarray

    def _L0_attn_setup():
        import jax, jax.numpy as jnp
        import numpy as np
        D_MODEL, D_STATE, D_CONV, EXPAND = (512, 16, 4, 2)
        D_INNER = EXPAND * D_MODEL
        B_SZ, L_SEQ = (2, 1024)
        key = jax.random.key(seed)
        ks = jax.random.split(key, 10)

        def xav(k, shape, gain=0.5):
            fan_in, fan_out = (shape[1], shape[0])
            a = gain * np.sqrt(6.0 / (fan_in + fan_out))
            return jax.random.uniform(k, shape, jnp.float32, -a, a)
        x = jax.random.normal(ks[0], (B_SZ, L_SEQ, D_MODEL), jnp.float32)
        ln_gamma = jnp.ones((D_MODEL,), jnp.float32)
        ln_beta = jnp.zeros((D_MODEL,), jnp.float32)
        W_in = xav(ks[1], (2 * D_INNER, D_MODEL))
        conv_w = jax.random.normal(ks[2], (D_INNER, 1, D_CONV), jnp.float32) * (1.0 / np.sqrt(D_CONV))
        conv_b = jax.random.uniform(ks[3], (D_INNER,), jnp.float32, -0.1, 0.1)
        A_log = jnp.log(jnp.tile(jnp.arange(1, D_STATE + 1, dtype=jnp.float32), (D_INNER, 1)))
        D_param = jax.random.uniform(ks[4], (D_INNER,), jnp.float32, -0.01, 0.01)
        W_xproj = xav(ks[5], (2 * D_STATE + 1, D_INNER))
        W_dt = xav(ks[6], (D_INNER, 2 * D_STATE + 1))
        b_dt = jnp.zeros((D_INNER,), jnp.float32)
        W_out = xav(ks[7], (D_MODEL, D_INNER))
        return {'x': x, 'ln_gamma': ln_gamma, 'ln_beta': ln_beta, 'W_in': W_in, 'conv_w': conv_w, 'conv_b': conv_b, 'A_log': A_log, 'D_param': D_param, 'W_xproj': W_xproj, 'W_dt': W_dt, 'b_dt': b_dt, 'W_out': W_out}
    _L0_attn_in = _L0_attn_setup()

    def _L0_ffn_setup():
        import jax, jax.numpy as jnp
        import numpy as np
        E = 8
        K = 2
        D = 512
        B, N = (4, 2048)
        DC = 256
        key = jax.random.key(seed)
        ks = jax.random.split(key, 6)
        x = jax.random.normal(ks[0], (B, N, D), jnp.float32)
        cond = jax.random.normal(ks[1], (B, N, DC), jnp.float32)
        mask = jnp.ones((B, N), jnp.float32)
        W_shared = jax.random.normal(ks[2], (D, D), jnp.float32) * 0.02
        W_expert = jax.random.normal(ks[3], (D, D), jnp.float32) * 0.02
        W_gate = jax.random.normal(ks[4], (D, E - 1), jnp.float32) * 0.02
        bias = jnp.zeros((D,), jnp.float32)
        return dict(x=x, cond=cond, mask=mask, W_shared=W_shared, W_expert=W_expert, W_gate=W_gate, bias=bias)
    _L0_ffn_in = _L0_ffn_setup()
    _d = {'L0_attn_x': _L0_attn_in['x'], 'L0_attn_ln_gamma': _L0_attn_in['ln_gamma'], 'L0_attn_ln_beta': _L0_attn_in['ln_beta'], 'L0_attn_W_in': _L0_attn_in['W_in'], 'L0_attn_conv_w': _L0_attn_in['conv_w'], 'L0_attn_conv_b': _L0_attn_in['conv_b'], 'L0_attn_A_log': _L0_attn_in['A_log'], 'L0_attn_D_param': _L0_attn_in['D_param'], 'L0_attn_W_xproj': _L0_attn_in['W_xproj'], 'L0_attn_W_dt': _L0_attn_in['W_dt'], 'L0_attn_b_dt': _L0_attn_in['b_dt'], 'L0_attn_W_out': _L0_attn_in['W_out'], 'L0_ffn_cond': _L0_ffn_in['cond'], 'L0_ffn_mask': _L0_ffn_in['mask'], 'L0_ffn_W_shared': _L0_ffn_in['W_shared'], 'L0_ffn_W_expert': _L0_ffn_in['W_expert'], 'L0_ffn_W_gate': _L0_ffn_in['W_gate'], 'L0_ffn_bias': _L0_ffn_in['bias']}
    _x0 = _d['L0_attn_x']
    _d['L0_attn_x'] = jax.random.normal(jax.random.fold_in(jax.random.key(seed), 1), (2, 4096, 512), dtype=_x0.dtype)
    del _x0
    return _d

def reference(L0_attn_x, L0_attn_ln_gamma, L0_attn_ln_beta, L0_attn_W_in, L0_attn_conv_w, L0_attn_conv_b, L0_attn_A_log, L0_attn_D_param, L0_attn_W_xproj, L0_attn_W_dt, L0_attn_b_dt, L0_attn_W_out, L0_ffn_cond, L0_ffn_mask, L0_ffn_W_shared, L0_ffn_W_expert, L0_ffn_W_gate, L0_ffn_bias):

    def _L0_attn_ref(x, ln_gamma, ln_beta, W_in, conv_w, conv_b, A_log, D_param, W_xproj, W_dt, b_dt, W_out):
        import jax, jax.numpy as jnp
        import numpy as np
        D_MODEL, D_STATE, D_CONV, EXPAND = (512, 16, 4, 2)
        D_INNER = EXPAND * D_MODEL
        B_SZ, L_SEQ = (2, 1024)
        B, L, Dm = x.shape
        Di, N = A_log.shape
        mu = jnp.mean(x, -1, keepdims=True)
        var = jnp.var(x, -1, keepdims=True)
        xn = (x - mu) * jax.lax.rsqrt(var + 1e-05) * ln_gamma + ln_beta
        xz = xn @ W_in.T
        x_ssm, z = (xz[..., :Di], xz[..., Di:])
        K = conv_w.shape[-1]
        xc = jnp.swapaxes(x_ssm, 1, 2)
        xc = jax.lax.conv_general_dilated(xc, conv_w, (1,), [(K - 1, 0)], dimension_numbers=('NCH', 'OIH', 'NCH'), feature_group_count=Di) + conv_b[None, :, None]
        x_ssm = jax.nn.silu(jnp.swapaxes(xc, 1, 2))
        xp = x_ssm @ W_xproj.T
        B_self = xp[..., 1:1 + N]
        C_self = xp[..., 1 + N:]
        dt = jax.nn.softplus(xp @ W_dt.T + b_dt) + 0.001
        A = -jnp.exp(A_log)

        def step(h, inp):
            x_t, dt_t, B_t, C_t = inp
            dA = jnp.exp(A[None] * dt_t[..., None])
            dB = (1.0 - dA) / (A[None] + 1e-08) * B_t[:, None, :]
            h = jnp.clip(dA * h + dB * x_t[..., None], -10.0, 10.0)
            y_t = jnp.sum(C_t[:, None, :] * h, -1) + D_param * x_t
            return (h, y_t)
        h0 = jnp.zeros((B, Di, N), x.dtype)
        xs = (jnp.swapaxes(x_ssm, 0, 1), jnp.swapaxes(dt, 0, 1), jnp.swapaxes(B_self, 0, 1), jnp.swapaxes(C_self, 0, 1))
        _, ys = jax.lax.scan(step, h0, xs)
        y = jnp.swapaxes(ys, 0, 1) * jax.nn.silu(z)
        return y @ W_out.T

    def _L0_ffn_ref(x, cond, mask, W_shared, W_expert, W_gate, bias):
        import jax, jax.numpy as jnp
        import numpy as np
        E = 8
        K = 2
        D = 512
        B, N = (4, 2048)
        DC = 256
        b, n, d = x.shape
        T = b * n
        xf = x.reshape(T, d)
        scores = jax.nn.softmax(xf @ W_gate, axis=-1)
        expert_weights, _ = jax.lax.top_k(scores, K)
        expert_weights = expert_weights / expert_weights.sum(-1, keepdims=True)
        expert_indices = (jnp.arange(T * K) % E).reshape(T, K)
        te = expert_indices.reshape(-1)
        w = expert_weights.reshape(-1)
        capacity = K * T // E
        order = jnp.argsort(te, stable=True)
        sorted_e = te[order]
        hist = jnp.bincount(te, length=E)
        starts = jnp.concatenate([jnp.zeros((1,), hist.dtype), jnp.cumsum(hist)[:-1]])
        pos = jnp.arange(T * K) - starts[sorted_e]
        valid = pos < capacity
        dest = jnp.where(valid, sorted_e * capacity + pos, E * capacity)
        tok = order // K
        gathered = jnp.zeros((E * capacity + 1, d), x.dtype).at[dest].set(xf[tok])
        gathered = gathered[:-1]
        y = gathered @ W_expert.T
        contrib = w[order][:, None] * y[jnp.minimum(dest, E * capacity - 1)]
        moe_out = jnp.zeros((T, d), x.dtype).at[tok].add(jnp.where(valid[:, None], contrib, 0.0))
        shared = xf @ W_shared.T
        out = (shared + moe_out + bias).reshape(b, n, d)
        return out
    x = L0_attn_x
    x = x + _L0_attn_ref(_layernorm(x, axis=-1), L0_attn_ln_gamma, L0_attn_ln_beta, L0_attn_W_in, L0_attn_conv_w, L0_attn_conv_b, L0_attn_A_log, L0_attn_D_param, L0_attn_W_xproj, L0_attn_W_dt, L0_attn_b_dt, L0_attn_W_out)
    x = x + _L0_ffn_ref(_layernorm(x, axis=-1), L0_ffn_cond, L0_ffn_mask, L0_ffn_W_shared, L0_ffn_W_expert, L0_ffn_W_gate, L0_ffn_bias)
    return x

_drawn_inputs = setup_inputs


def setup_inputs(seed=0):
    import zlib

    import numpy as np

    out = dict(_drawn_inputs(seed))
    spreads = {'L0_attn_ln_gamma': (1.0, 0.2),
     'L0_attn_ln_beta': (0.0, 0.1),
     'L0_attn_b_dt': (0.0, 0.1),
     'L0_ffn_bias': (0.0, 0.1)}
    factors = {}
    for name, (base, spread) in spreads.items():
        noise = np.random.default_rng([zlib.crc32(name.encode()), seed]).standard_normal(out[name].shape)
        drawn = base * np.exp(spread * noise) if base else spread * noise
        out[name] = jnp.asarray(drawn.astype(out[name].dtype))
    for name, factor in factors.items():
        out[name] = (out[name] * factor).astype(out[name].dtype)
    return out
```

```python
import concourse.bass as bass
from concourse import mybir
from contextlib import ExitStack

P = 128
BATCH, LEN, DM = 2, 4096, 512
DI, NS, TAPS, NX = 1024, 16, 4, 33
TOKENS = BATCH * LEN
CH = 512
NCH = LEN // CH
KD = DM // P
MD = DI // P
SUB = CH // P
GRP = CH // 64
GATES, TOPK = 7, 2
EPS = 1e-5
PAD = LEN + 1

W_DIAG, W_INVT, W_A, W_D, W_LIM = 0, NS * P, NS * P + P, NS * P + P + NS, NS * P + P + NS + 1
W_COLS = W_LIM + NS

F32 = mybir.dt.float32
I32 = mybir.dt.int32
ALU = mybir.AluOpType
ACT = mybir.ActivationFunctionType
AX = mybir.AxisListType


def bcast(ap, dims):
    return bass.AP(tensor=ap.tensor, offset=ap.offset, ap=[tuple(ap.ap[0])] + dims)


def build(nc, t_in, out):
    with ExitStack() as ctx:
        def sb(name, shape, dt=F32, c=None):
            return (c or ctx).enter_context(nc.sbuf_tensor(name, shape, dt))

        def sem(name, c=None):
            return (c or ctx).enter_context(nc.semaphore(name))

        xs_d = nc.dram_tensor("xs_d", [BATCH, MD, P, PAD], F32).ap()
        dt_d = nc.dram_tensor("dt_d", [BATCH, MD, P, LEN], F32).ap()
        zs_d = nc.dram_tensor("zs_d", [BATCH, MD, P, LEN], F32).ap()
        xp_d = nc.dram_tensor("xp_d", [BATCH, NX, PAD], F32).ap()
        w_d = nc.dram_tensor("w_d", [MD, P, W_COLS], F32).ap()
        x1_d = nc.dram_tensor("x1_d", [TOKENS, DM], F32).ap()

        ident = sb("ident", [P, P])
        mask_d = sb("mask_d", [P, 32])
        minus_half = sb("minus_half", [P, SUB])
        clips = sb("clips", [1, 1], I32)
        with ExitStack() as early:
            ones = sb("ones", [P, P], c=early)
            margin = sb("margin", [P, MD, NS], c=early)
            within = sb("within", [P, MD, NS], c=early)
            setup(nc, sb, sem, t_in, ident, ones, mask_d, minus_half, margin, within, xs_d, xp_d, w_d)
            front(nc, sb, sem, t_in, ident, ones, minus_half, margin, within, clips, xs_d, dt_d, zs_d, xp_d)
        scan(nc, sb, sem, t_in, ident, mask_d, clips, xs_d, dt_d, zs_d, xp_d, w_d, x1_d)
        ffn(nc, sb, sem, t_in, ident, minus_half, x1_d, out)


def setup(nc, sb, sem, t_in, ident, ones, mask_d, minus_half, margin, within, xs_d, xp_d, w_d):
    with ExitStack() as c:
        zeros = sb("zeros", [P, 16], c=c)
        a_log = sb("a_log", [P, MD, NS], c=c)
        ea = sb("ea", [P, MD, NS], c=c)
        ap_ = sb("ap_", [P, MD, NS], c=c)
        an = sb("an", [P, MD, NS], c=c)
        inv = sb("inv", [P, MD, NS], c=c)
        d_par = sb("d_par", [P, MD], c=c)
        w = sb("w", [P, 2, W_COLS], c=c)
        ps = c.enter_context(nc.psum_tensor("ps_setup", [NS, MD, P], F32))
        s_in, s_pool, s_exp, s_dve = sem("su_in", c), sem("su_pool", c), sem("su_exp", c), sem("su_dve", c)
        s_tr, s_w, s_zero = sem("su_tr", c), sem("su_w", c), sem("su_zero", c)
        s_wo = [sem(f"su_wo{i}", c) for i in range(2)]

        with nc.Block() as block:
            @block.sync
            def _(sp):
                sp.dma_start(a_log[:, :, :], t_in["A_log"].rearrange("(m p) n -> p m n", p=P)).then_inc(s_in, 16)
                sp.dma_start(d_par[:, :], t_in["D_param"]).then_inc(s_in, 16)
                sp.wait_ge(s_pool, 1)
                for b in range(BATCH):
                    sp.dma_start(xs_d[b, :, :, 0:1].rearrange("m p o -> p m o"), zeros[:, 0:MD],
                                 allow_slow_non_contiguous=True).then_inc(s_zero, 16)
                    sp.dma_start(xp_d[b, :, 0:1], zeros[0:NX, 0:1],
                                 allow_slow_non_contiguous=True).then_inc(s_zero, 16)
                for m in range(MD):
                    sp.wait_ge(s_w, m + 1)
                    sp.dma_start(w_d[m, :, :], w[:, m % 2, :]).then_inc(s_wo[m % 2], 16)
                for i in range(2):
                    sp.wait_ge(s_wo[i], 16 * MD // 2)
                sp.wait_ge(s_zero, 16 * 2 * BATCH)

            @block.gpsimd
            def _(pool):
                pool.memset(zeros[:, :], 0.0).then_inc(s_pool, 1)
                pool.memset(ident[:, :], 0.0).then_inc(s_pool, 1)
                pool.memset(mask_d[:, :], 0.0).then_inc(s_pool, 1)
                pool.memset(ones[:, :], 1.0).then_inc(s_pool, 1)
                pool.memset(minus_half[:, :], -0.5).then_inc(s_pool, 1)
                pool.memset(within[:, :, :], 1.0).then_inc(s_pool, 1)
                pool.wait_ge(s_pool, 6)
                pool.affine_select(out=ident[:, :], in_=ident[:, :], compare_op=ALU.not_equal, fill=1.0,
                                   base=0, pattern=[[-1, P]], channel_multiplier=1).then_inc(s_pool, 1)
                for k in range(4):
                    pool.affine_select(out=mask_d[:, :], in_=mask_d[:, :], compare_op=ALU.not_equal,
                                       fill=1.0 if k % 2 == 0 else -1.0, base=-32 * k, pattern=[[-1, 32]],
                                       channel_multiplier=1).then_inc(s_pool, 1)
                    pool.wait_ge(s_pool, 8 + k)

            @block.scalar
            def _(act):
                act.wait_ge(s_in, 32)
                act.activation(ea[:, :, :], a_log[:, :, :], ACT.Exp).then_inc(s_exp, 1)

            @block.tensor
            def _(pe):
                pe.wait_ge(s_pool, 7)
                pe.wait_ge(s_dve, 4)
                for m in range(MD):
                    last = pe.transpose(ps[:, m, :], inv[:, m, :], ident[:, :])
                last.then_inc(s_tr, 1)

            @block.vector
            def _(dve):
                done = [0]

                def step(ins):
                    done[0] += 1
                    ins.then_inc(s_dve, 1)
                    dve.wait_ge(s_dve, done[0])
                dve.wait_ge(s_exp, 1)
                step(dve.tensor_scalar(ap_[:, :, :], ea[:, :, :], -1.0, 1e-8, ALU.mult, ALU.add))
                step(dve.tensor_scalar(an[:, :, :], ap_[:, :, :], -1.0, None, ALU.mult))
                step(dve.tensor_tensor(an[:, :, :], an[:, :, :], ap_[:, :, :], ALU.max))
                step(dve.reciprocal(inv[:, :, :], ap_[:, :, :]))
                step(dve.tensor_scalar(margin[:, :, :], an[:, :, :], 9.9, None, ALU.mult))
                step(dve.memset(w[:, :, :], 0.0))
                dve.wait_ge(s_pool, 7)
                dve.wait_ge(s_tr, 1)
                for m in range(MD):
                    e = m % 2
                    if m >= 2:
                        dve.wait_ge(s_wo[e], 16 * (m // 2))
                    step(dve.tensor_tensor(w[:, e, W_DIAG:W_DIAG + NS * P].rearrange("p (n k) -> p n k", n=NS),
                                           bcast(ident[:, :], [(0, NS), (1, P)]),
                                           bcast(inv[:, m, :], [(1, NS), (0, P)]), ALU.mult))
                    step(dve.tensor_copy(w[0:NS, e, W_INVT:W_INVT + P], ps[:, m, :]))
                    step(dve.tensor_scalar(w[:, e, W_A:W_A + NS], ea[:, m, :], -1.0, None, ALU.mult))
                    step(dve.tensor_copy(w[:, e, W_D:W_D + 1], d_par[:, m:m + 1]))
                    step(dve.tensor_scalar(w[:, e, W_LIM:W_LIM + NS], an[:, m, :], 10.0, None, ALU.mult))
                    dve.sem_inc(s_w, 1)


def front(nc, sb, sem, t_in, ident, ones, minus_half, margin, within, clips, xs_d, dt_d, zs_d, xp_d):
    HALO = TAPS - 1
    RING = 4
    with ExitStack() as c:
        w_in = sb("w_in", [P, KD, 2 * DI], c=c)
        w_xp = sb("w_xp", [P, MD, NX], c=c)
        w_dt = sb("w_dt", [NX, DI], c=c)
        gamma, beta = sb("gamma", [P, KD], c=c), sb("beta", [P, KD], c=c)
        taps, cbias, bdt = sb("taps", [P, MD, TAPS], c=c), sb("cbias", [P, MD], c=c), sb("bdt", [P, MD], c=c)
        x = sb("x_f", [P, SUB, DM], c=c)
        stats, mv = sb("stats_f", [P, SUB, 6], c=c), sb("mv_f", [P, SUB, 2], c=c)
        spread, rstd = sb("spread_f", [P, SUB], c=c), sb("rstd_f", [P, SUB], c=c)
        xn = sb("xn_f", [P, SUB, DM], c=c)
        xnt = sb("xnt_f", [P, KD, CH], c=c)
        xz = sb("xz", [P, MD, HALO + CH], c=c)
        conv = sb("conv", [P, 2, CH], c=c)
        zs = sb("zs_f", [P, RING, CH], c=c)
        xs = sb("xs_f", [P, MD, CH], c=c)
        xp = sb("xp_f", [NX, CH], c=c)
        v = sb("v_f", [P, MD, CH], c=c)
        lg = sb("lg_f", [P, MD, CH], c=c)
        xmax, bmax = sb("xmax", [P, MD], c=c), sb("bmax", [NX, 1], c=c)
        bdiag = sb("bdiag", [NX, NX], c=c)
        umax, inside = sb("umax", [P, MD, NS], c=c), sb("inside", [P, MD, NS], c=c)
        inside1 = sb("inside1", [P, 1], c=c)
        ps_t = c.enter_context(nc.psum_tensor("ps_t_f", [P, 2, CH], F32))
        ps_r = c.enter_context(nc.psum_tensor("ps_r_f", [P, RING, CH], F32))
        ps_xp = c.enter_context(nc.psum_tensor("ps_xp", [P, CH], F32))
        ps_b = c.enter_context(nc.psum_tensor("ps_b", [P, CH], F32))

        S = lambda n: sem("f_" + n, c)
        s_wt, s_x, s_one = S("weights"), S("x"), S("one")
        s_st, s_pow, s_xn, s_tr, s_te = S("stats"), S("pow"), S("xn"), S("tr"), S("te")
        s_mm, s_xe, s_z, s_cv, s_xs = S("mm"), S("xe"), S("z"), S("cv"), S("xs")
        s_halo, s_xm, s_xpm, s_xpe, s_xpo = S("halo"), S("xm"), S("xpm"), S("xpe"), S("xpo")
        s_v, s_l, s_r, s_dt, s_dto, s_xso = S("v"), S("l"), S("r"), S("dt"), S("dto"), S("xso")
        s_zo = [S(f"zo{i}") for i in range(RING)]
        s_pass, s_bd, s_bb, s_in, s_fl = S("pass"), S("bd"), S("bb"), S("in"), S("flag")

        with nc.Block() as block:
            @block.sync
            def _(sp):
                for dst, src in ((w_in[:, :, :], t_in["W_inT"].rearrange("(k p) n -> p k n", p=P)),
                                 (w_xp[:, :, :], t_in["W_xprojT"].rearrange("(k p) n -> p k n", p=P)),
                                 (w_dt[:, :], t_in["W_dtT"]),
                                 (gamma[:, :], t_in["ln_gamma"]),
                                 (beta[:, :], t_in["ln_beta"]),
                                 (taps[:, :, :], t_in["conv_w"].rearrange("(m p) k -> p m k", p=P)),
                                 (cbias[:, :], t_in["conv_b"]),
                                 (bdt[:, :], t_in["b_dt"])):
                    sp.dma_start(dst, src).then_inc(s_wt, 16)
                sp.dma_start(x[:, :, :], t_in["x"][0:CH, :].rearrange("(s p) d -> p s d", p=P)).then_inc(s_x, 16)
                with sp.Fori(0, BATCH) as b:
                    with sp.Fori(0, NCH) as k:
                        ch = b * NCH + k
                        after = (ch + 1) % (BATCH * NCH)
                        sp.wait_ge(s_xn, ch * SUB + SUB)
                        sp.dma_start(x[:, :, :], t_in["x"][bass.ts(after, CH), :].rearrange("(s p) d -> p s d", p=P))\
                            .then_inc(s_x, 16)
                        sp.wait_ge(s_xpe, ch + 1)
                        sp.dma_start(xp_d[b, :, bass.ds(k * CH + 1, CH)], xp[:, :]).then_inc(s_xpo, 16)
                        for h in range(2):
                            m0, m1 = h * MD // 2, (h + 1) * MD // 2
                            sp.wait_ge(s_dt, ch * 2 + h + 2)
                            sp.dma_start(dt_d[b, m0:m1, :, bass.ts(k, CH)].rearrange("m p t -> p m t"),
                                         lg[:, m0:m1, :]).then_inc(s_dto, 16)
                sp.wait_ge(s_x, 16 * (BATCH * NCH + 1))
                sp.wait_ge(s_xpo, BATCH * NCH * 16 + 1)
                sp.wait_ge(s_dto, BATCH * NCH * 32 + 1)

            @block.gpsimd
            def _(pool):
                pool.sem_inc(s_xpo, 1)
                pool.sem_inc(s_dto, 1)
                pool.sem_inc(s_xso, 1)
                pool.sem_inc(s_dt, 1)
                pool.sem_inc(s_xm, 1)
                pool.sem_inc(s_v, RING)
                for i in range(RING):
                    pool.sem_inc(s_zo[i], 1)
                with pool.Fori(0, BATCH * NCH) as ch:
                    pool.wait_ge(s_st, ch + 1)
                    pool.tensor_tensor(rstd[:, :], spread[:, :], minus_half[:, :], ALU.pow).then_inc(s_pow, 1)
                    for h in range(2):
                        m0, m1 = h * MD // 2, (h + 1) * MD // 2
                        pool.wait_ge(s_l, ch * 6 + 3 * h + 1)
                        pool.sem_inc(s_pass, 1)
                        pool.tensor_scalar(v[:, m0:m1, :], v[:, m0:m1, :], 0.0, 1e-3, ALU.max, ALU.add)\
                            .then_inc(s_r, 1)
                        pool.wait_ge(s_r, ch * 2 + h + 1)
                        pool.wait_ge(s_l, ch * 6 + 3 * h + 3)
                        pool.tensor_tensor(lg[:, m0:m1, :], lg[:, m0:m1, :], v[:, m0:m1, :], ALU.add)\
                            .then_inc(s_dt, 1)

            @block.scalar
            def _(act):
                act.wait_ge(s_wt, 8 * 16)
                with act.Fori(0, BATCH) as b:
                    with act.Fori(0, NCH) as k:
                        ch = b * NCH + k
                        for q in range(KD):
                            act.wait_ge(s_tr, ch * KD + q + 1)
                            act.activation(xnt[:, q, :], ps_t[:, q % 2, :], ACT.Identity,
                                           scale=gamma[:, q:q + 1], bias=beta[:, q:q + 1]).then_inc(s_te, 1)
                        act.wait_ge(s_halo, ch + b + 1)
                        for m in range(MD):
                            act.wait_ge(s_mm, ch * 24 + m + 1)
                            act.activation(xz[:, m, HALO:HALO + CH], ps_r[:, m % RING, :], ACT.Copy).then_inc(s_xe, 1)
                        act.wait_ge(s_xm, ch + 1)
                        act.wait_ge(s_xso, ch * (16 * MD) + 1)
                        for m in range(MD):
                            act.wait_ge(s_mm, ch * 24 + MD + m + 1)
                            act.wait_ge(s_zo[m % RING], ch * 32 + (m // RING) * 16 + 1)
                            act.activation(zs[:, m % RING, :], ps_r[:, m % RING, :], ACT.Silu).then_inc(s_z, 1)
                            act.wait_ge(s_z, ch * MD + m + 1)
                            act.dma_start(zs_d[b, m, :, bass.ts(k, CH)], zs[:, m % RING, :]).then_inc(s_zo[m % RING], 16)
                            act.wait_ge(s_cv, ch * 32 + 4 * m + 4)
                            act.activation(xs[:, m, :], conv[:, m % 2, :], ACT.Silu).then_inc(s_xs, 1)
                            act.wait_ge(s_xs, ch * MD + m + 1)
                            act.dma_start(xs_d[b, m, :, bass.ds(k * CH + 1, CH)], xs[:, m, :]).then_inc(s_xso, 16)
                        act.wait_ge(s_dto, ch * 32 + 1)
                        for h in range(2):
                            m0, m1 = h * MD // 2, (h + 1) * MD // 2
                            act.wait_ge(s_v, ch * MD + m1 + RING)
                            act.activation(lg[:, m0:m1, :], v[:, m0:m1, :], ACT.Abs).then_inc(s_l, 1)
                            act.wait_ge(s_l, ch * 6 + 3 * h + 1)
                            act.activation(lg[:, m0:m1, :], lg[:, m0:m1, :], ACT.Exp, scale=-1.0).then_inc(s_l, 1)
                            act.wait_ge(s_l, ch * 6 + 3 * h + 2)
                            act.activation(lg[:, m0:m1, :], lg[:, m0:m1, :], ACT.Ln, bias=1.0).then_inc(s_l, 1)
                act.wait_ge(s_xso, BATCH * NCH * MD * 16 + 1)
                for i in range(RING):
                    act.wait_ge(s_zo[i], BATCH * NCH * 32 + 1)

            @block.tensor
            def _(pe):
                pe.wait_ge(s_wt, 8 * 16)
                with pe.Fori(0, BATCH * NCH) as ch:
                    for q in range(KD):
                        if q >= 2:
                            pe.wait_ge(s_te, ch * KD + q - 1)
                        for s in range(SUB):
                            if q == 0:
                                pe.wait_ge(s_xn, ch * SUB + s + 1)
                            last = pe.transpose(ps_t[:, q % 2, s * P:(s + 1) * P], xn[:, s, q * P:(q + 1) * P],
                                                ident[:, :])
                        last.then_inc(s_tr, 1)
                    for r in range(2 * MD):
                        if r < RING:
                            pe.wait_ge(s_v, ch * MD + r + 1)
                        elif r < RING + MD:
                            pe.wait_ge(s_xe, ch * MD + r - RING + 1)
                        else:
                            pe.wait_ge(s_z, ch * MD + r - RING - MD + 1)
                        for q in range(KD):
                            if r == 0:
                                pe.wait_ge(s_te, ch * KD + q + 1)
                            last = pe.matmul(ps_r[:, r % RING, :], w_in[:, q, r * P:(r + 1) * P], xnt[:, q, :],
                                             start=(q == 0), stop=(q == KD - 1))
                        last.then_inc(s_mm, 1)
                    for m in range(MD):
                        pe.wait_ge(s_xs, ch * MD + m + 1)
                        last = pe.matmul(ps_xp[0:NX, :], w_xp[:, m, :], xs[:, m, :], start=(m == 0), stop=(m == MD - 1))
                    last.then_inc(s_xpm, 1)
                    pe.wait_ge(s_xpe, ch + 1)
                    for m in range(MD):
                        r = 2 * MD + m
                        if m < RING:
                            pe.wait_ge(s_z, ch * MD + m + RING + 1)
                        else:
                            pe.wait_ge(s_v, ch * MD + m - RING + 1 + RING)
                        pe.matmul(ps_r[:, r % RING, :], w_dt[:, m * P:(m + 1) * P], xp[:, :], start=True, stop=True)\
                            .then_inc(s_mm, 1)
                    pe.wait_ge(s_bd, ch + 1)
                    pe.matmul(ps_b[:, 0:NX], ones[0:NX, :], bdiag[:, :], start=True, stop=True).then_inc(s_bb, 1)
                pe.wait_ge(s_fl, 1)
                pe.matmul(ps_b[0:1, 0:1], ones[:, 0:1], inside1[:, :], start=True, stop=True).then_inc(s_fl, 1)

            @block.vector
            def _(dve):
                dve.wait_ge(s_wt, 8 * 16)
                with dve.Fori(0, BATCH) as b:
                    dve.memset(xz[:, :, 0:HALO], 0.0).then_inc(s_halo, 1)
                    with dve.Fori(0, NCH) as k:
                        ch = b * NCH + k
                        dve.wait_ge(s_x, ch * 16 + 16)
                        for s in range(SUB):
                            dve.bn_stats(stats[:, s, :], x[:, s, :]).then_inc(s_one, 1)
                        for s in range(SUB):
                            dve.wait_ge(s_one, ch * 8 + s + 1)
                            dve.sem_inc(s_pass, 1)
                            dve.bn_aggr(mv[:, s, :], stats[:, s, :]).then_inc(s_one, 1)
                        dve.wait_ge(s_one, ch * 8 + 8)
                        dve.tensor_scalar(spread[:, :], mv[:, :, 1], 1.0 + EPS, EPS * EPS, ALU.mult, ALU.add)\
                            .then_inc(s_st, 1)
                        dve.wait_ge(s_pow, ch + 1)
                        for s in range(SUB):
                            dve.tensor_scalar(xn[:, s, :], x[:, s, :], mv[:, s, 0:1], rstd[:, s:s + 1],
                                              ALU.subtract, ALU.mult).then_inc(s_xn, 1)
                        dve.wait_ge(s_halo, ch + b + 1)
                        for m in range(MD):
                            dve.wait_ge(s_xe, ch * MD + m + 1)
                            if m >= 2:
                                dve.wait_ge(s_xs, ch * MD + m - 1)
                            acc = conv[:, m % 2, :]
                            dve.tensor_scalar(acc, xz[:, m, 0:CH], taps[:, m, 0:1], cbias[:, m:m + 1],
                                              ALU.mult, ALU.add).then_inc(s_cv, 1)
                            for j in range(1, TAPS):
                                dve.wait_ge(s_cv, ch * 32 + 4 * m + j)
                                dve.scalar_tensor_tensor(acc, xz[:, m, j:j + CH], taps[:, m, j:j + 1], acc,
                                                         ALU.mult, ALU.add).then_inc(s_cv, 1)
                        dve.tensor_copy(xz[:, :, 0:HALO], xz[:, :, CH:CH + HALO]).then_inc(s_halo, 1)
                        dve.wait_ge(s_xs, ch * MD + MD)
                        dve.tensor_reduce(xmax[:, :], xs[:, :, :], AX.X, ALU.max, apply_absolute_value=True)\
                            .then_inc(s_xm, 1)
                        dve.wait_ge(s_xpm, ch + 1)
                        dve.wait_ge(s_xpo, ch * 16 + 1)
                        dve.tensor_copy(xp[:, :], ps_xp[0:NX, :]).then_inc(s_xpe, 1)
                        dve.wait_ge(s_dt, ch * 2 + 1)
                        for m in range(MD):
                            dve.wait_ge(s_mm, ch * 24 + 2 * MD + m + 1)
                            dve.tensor_scalar(v[:, m, :], ps_r[:, m % RING, :], bdt[:, m:m + 1], None, ALU.add)\
                                .then_inc(s_v, 1)
                        dve.wait_ge(s_xpe, ch + 1)
                        dve.tensor_reduce(bmax[:, :], xp[:, :], AX.X, ALU.max, apply_absolute_value=True).then_inc(s_in, 1)
                        dve.wait_ge(s_in, ch * 4 + 1)
                        dve.tensor_scalar(bdiag[:, :], ident[0:NX, 0:NX], bmax[:, 0:1], None, ALU.mult).then_inc(s_bd, 1)
                        dve.wait_ge(s_bb, ch + 1)
                        dve.wait_ge(s_xm, ch + 2)
                        dve.tensor_tensor(umax[:, :, :], bcast(xmax[:, :], [(1, MD), (0, NS)]),
                                          bcast(ps_b[:, 1:1 + NS], [(0, MD), (1, NS)]), ALU.mult).then_inc(s_in, 1)
                        dve.wait_ge(s_in, ch * 4 + 2)
                        dve.tensor_tensor(inside[:, :, :], umax[:, :, :], margin[:, :, :], ALU.is_le).then_inc(s_in, 1)
                        dve.wait_ge(s_in, ch * 4 + 3)
                        dve.tensor_tensor(within[:, :, :], within[:, :, :], inside[:, :, :], ALU.min).then_inc(s_in, 1)
                        dve.wait_ge(s_in, ch * 4 + 4)
                dve.tensor_reduce(inside1[:, :], within[:, :, :], AX.XY, ALU.min).then_inc(s_fl, 1)
                dve.wait_ge(s_fl, 2)
                dve.tensor_scalar(clips[:, :], ps_b[0:1, 0:1], P - 0.5, None, ALU.is_lt).then_inc(s_fl, 1)
                dve.wait_ge(s_fl, 3)


def scan(nc, sb, sem, t_in, ident, mask_d, clips, xs_d, dt_d, zs_d, xp_d, w_d, x1_d):
    STEPS = MD * NS
    XB, GB, QB = 3, 4, 5
    LAG = 3
    with ExitStack() as c:
        w = sb("w_s", [P, 2, W_COLS], c=c)
        xs, dt, zs = sb("xs_s", [P, XB, CH + 1], c=c), sb("dt_s", [P, 2, CH], c=c), sb("zs_s", [P, 2, CH], c=c)
        cc = sb("cc", [P, NS, CH], c=c)
        dm = sb("dm", [P, GRP, NS, 32], c=c)
        dd = sb("dd", [P, NS, CH], c=c)
        xd = sb("xd", [P, GRP, 2, 2, 32], c=c)
        xt = sb("xt", [P, 2, GRP, P], c=c)
        g, q = sb("g", [P, GB, CH], c=c), sb("q", [P, QB, CH], c=c)
        carry = sb("carry", [P, MD, NS], c=c)
        y = sb("y", [P, MD, CH], c=c)
        skip = sb("skip", [P, 2, CH], c=c)
        w_out = sb("w_out", [P, MD, DM], c=c)
        res = sb("res", [P, SUB, DM], c=c)
        xpd = sb("xpd", [NX, 2 * CH], c=c)
        b_r, c_r, bc = sb("b_r", [NS, CH], c=c), sb("c_r", [NS, CH], c=c), sb("bc", [NS, CH], c=c)
        b_ahead = sb("b_ahead", [P, NS], c=c)
        neg_u0 = sb("neg_u0", [P, NS], c=c)
        neg_u = sb("neg_u", [P, CH], c=c)
        fac, lim = sb("fac", [P, CH, 2], c=c), sb("lim", [P, CH, 2], c=c)
        ps_a = c.enter_context(nc.psum_tensor("ps_a", [P, 2, CH], F32))
        ps_d = c.enter_context(nc.psum_tensor("ps_d", [P, 2, 2, 8, 32], F32))
        ps_y = c.enter_context(nc.psum_tensor("ps_y", [P, 2, CH], F32))
        ps_x = c.enter_context(nc.psum_tensor("ps_x", [P, CH], F32))
        ps_m = c.enter_context(nc.psum_tensor("ps_m", [P, CH], F32))

        S = lambda n: sem("s_" + n, c)
        s_pass = S("pass")
        s_wt, s_xpl, s_ba, s_bt, s_dm, s_skp = S("weights"), S("xpl"), S("ba"), S("bt"), S("dm"), S("skip")
        s_slot, s_cc = [S("slot0"), S("slot1")], [S(f"cc{i}") for i in range(4)]
        s_xsl = [S(f"xsl{i}") for i in range(XB)]
        s_xd, s_tr, s_xt, s_dps, s_dd = S("xd"), S("tr"), S("xt"), S("dps"), S("dd")
        s_a, s_g, s_q, s_n, s_fin, s_half, s_bcm = S("a"), S("g"), S("q"), S("n"), S("fin"), S("half"), S("bcm")
        s_car, s_o, s_oe, s_res, s_out, s_slow = S("carry"), S("o"), S("oe"), S("res"), S("out"), S("slow")
        C_DM, C_FIN, C_Q, C_OE, C_OUT = 1, XB, NS, 1, 1

        def x_loads(ch, m):
            return ch * (16 * len(range(m % XB, MD, XB))) + 16 * (m // XB) + 16

        with nc.Block() as block:
            @block.sync
            def _(sp):
                sp.dma_start(w_out[:, :, :], t_in["W_outT"].rearrange("(m p) n -> p m n", p=P)).then_inc(s_wt, 16)
                with sp.Fori(0, BATCH) as b:
                    with sp.Fori(0, NCH) as k:
                        ch = b * NCH + k
                        sp.wait_ge(s_dm, ch * 3 + C_DM)
                        for early in range(2):
                            sp.dma_start(xpd[:, :].rearrange("p (b s j) -> p b s j", s=2, j=32)[:, :, early, :],
                                         xp_d[b, :, bass.ds(k * CH + early, CH)].rearrange("p (b j) -> p b j", j=32))\
                                .then_inc(s_xpl, 16)
                        sp.dma_start(b_r[:, :], xp_d[b, 1:1 + NS, bass.ds(k * CH + 1, CH)]).then_inc(s_xpl, 16)
                        sp.dma_start(c_r[:, :], xp_d[b, 1 + NS:NX, bass.ds(k * CH + 1, CH)]).then_inc(s_xpl, 16)
                        for m in range(MD):
                            sp.wait_ge(s_fin, ch * MD + m - 1 + C_FIN)
                            e = m % 2
                            sp.dma_start(dt[:, e, :], dt_d[b, m, :, bass.ts(k, CH)]).then_inc(s_slot[e], 16)
                            sp.dma_start(w[:, e, :], w_d[m, :, :]).then_inc(s_slot[e], 16)
                            sp.dma_start(zs[:, e, :], zs_d[b, m, :, bass.ts(k, CH)]).then_inc(s_slot[e], 16)
                            if m == 0:
                                for i in range(4):
                                    sp.wait_ge(s_q, ch * STEPS + 4 * i + 4 - NS + C_Q)
                                    row = xp_d[b, 1 + NS + 4 * i:5 + NS + 4 * i, bass.ds(k * CH + 1, CH)]
                                    sp.dma_start(cc[:, 4 * i:4 * i + 4, :], row.partition_broadcast(P))\
                                        .then_inc(s_cc[i], 16)
                            if m == 1:
                                row = xp_d[b, 1:1 + NS, bass.ds(k * CH, 1)].rearrange("n o -> (n o)")
                                sp.dma_start(b_ahead[:, :], row.partition_broadcast(P),
                                             allow_slow_non_contiguous=True).then_inc(s_ba, 16)

            @block.gpsimd
            def _(pool):
                pool.sem_inc(s_dm, C_DM)
                pool.sem_inc(s_fin, C_FIN)
                pool.sem_inc(s_q, C_Q)
                pool.sem_inc(s_oe, C_OE)
                pool.sem_inc(s_out, C_OUT)
                with pool.Fori(0, BATCH * NCH) as ch:
                    for s in range(STEPS):
                        n = s % NS
                        if s < NS and n % 4 == 0:
                            pool.wait_ge(s_cc[n // 4], ch * 16 + 16)
                        pool.wait_ge(s_g, ch * STEPS + s + 1)
                        if s >= QB:
                            pool.wait_ge(s_n, ch * STEPS + s - QB + 1)
                        pool.tensor_tensor(q[:, s % QB, :], g[:, s % GB, :], cc[:, n, :], ALU.mult).then_inc(s_q, 1)

            @block.scalar
            def _(act):
                with act.Fori(0, BATCH) as b:
                    with act.Fori(0, NCH) as k:
                        ch = b * NCH + k

                        def load_x(m):
                            act.wait_ge(s_fin, ch * MD + m + 1 - XB + C_FIN)
                            act.dma_start(xs[:, m % XB, :], xs_d[b, m, :, bass.ds(k * CH, CH + 1)])\
                                .then_inc(s_xsl[m % XB], 16)

                        def double_x(m):
                            act.wait_ge(s_xsl[m % XB], x_loads(ch, m))
                            act.activation(xd[:, :, :, :, :].rearrange("p g b s j -> p (g b) s j"),
                                           bcast(xs[:, m % XB, 0:1], [(32, 2 * GRP), (1, 2), (1, 32)]), ACT.Copy)\
                                .then_inc(s_xd, 1)

                        def turned(m, p):
                            act.wait_ge(s_tr, ch * (2 * MD) + 2 * m + p + 1)
                            act.activation(xt[:, m % 2, 4 * p:4 * p + 4, :], ps_x[:, :], ACT.Copy).then_inc(s_xt, 1)

                        def move_d(half, i):
                            if i == 0 and half >= 2:
                                act.wait_ge(s_g, ch * STEPS + 8 * (half - 1))
                            act.wait_ge(s_dps, ch * STEPS + 8 * half + i + 1)
                            n0, t0 = 8 * (half % 2), 128 * (i // 2) + 32 * (i % 2)
                            act.activation(bcast(dd[:, n0, t0:t0 + 1], [(64, 2), (CH, 8), (1, 32)]),
                                           ps_d[:, i % 2, :, :, :], ACT.Copy).then_inc(s_dd, 1)

                        load_x(0)
                        load_x(1)
                        act.wait_ge(s_out, ch * 16 + C_OUT)
                        act.dma_start(res[:, :, :], t_in["x"][bass.ts(ch, CH), :].rearrange("(s p) d -> p s d", p=P))\
                            .then_inc(s_res, 16)
                        double_x(0)
                        for p in range(2):
                            turned(0, p)
                        for i in range(8):
                            move_d(0, i)
                        for m in range(MD):
                            e = m % 2
                            act.wait_ge(s_slot[e], ch * 192 + 48 * (m // 2) + 48)
                            for n in range(NS):
                                s = m * NS + n
                                if s >= 2:
                                    act.wait_ge(s_g, ch * STEPS + s - 1)
                                act.activation(ps_a[:, n % 2, :], dt[:, e, :], ACT.Exp,
                                               scale=w[:, e, W_A + n:W_A + n + 1]).then_inc(s_a, 1)
                                half = 2 * m + n // 8 + 1
                                if m + 1 < MD and n == 0:
                                    double_x(m + 1)
                                if m + 2 < MD and n == 9:
                                    load_x(m + 2)
                                if m + 1 < MD and n in (3, 6):
                                    turned(m + 1, n // 4)
                                if half < 2 * MD:
                                    move_d(half, n % 8)
                        act.wait_ge(s_oe, ch * SUB + SUB + C_OE)
                        act.dma_start(x1_d[bass.ts(ch, CH), :].rearrange("(s p) d -> p s d", p=P), res[:, :, :])\
                            .then_inc(s_out, 16)
                act.wait_ge(s_out, BATCH * NCH * 16 + C_OUT)

            @block.tensor
            def _(pe):
                pe.wait_ge(s_wt, 16)
                with pe.Fori(0, BATCH * NCH) as ch:
                    def turn(m, p):
                        if p == 0:
                            pe.wait_ge(s_xd, ch * MD + m + 1)
                        if 2 * m + p > 0:
                            pe.wait_ge(s_xt, ch * (2 * MD) + 2 * m + p)
                        for i in range(4):
                            last = pe.transpose(ps_x[:, i * P:(i + 1) * P],
                                                xd[:, 4 * p + i, :, :, :].rearrange("p b s j -> p (b s j)"), ident[:, :])
                        last.then_inc(s_tr, 1)

                    def make_d(half, pair):
                        m, n0 = half // 2, 8 * (half % 2)
                        if half + pair > 0:
                            pe.wait_ge(s_dd, ch * STEPS + 8 * half + 2 * pair)
                        if half % 2 == 0:
                            pe.wait_ge(s_xt, ch * (2 * MD) + 2 * m + pair // 2 + 1)
                        for i in range(2):
                            for r in range(2):
                                rows, grp = slice(64 * r, 64 * r + 64), 2 * pair + i
                                last = pe.matmul(ps_d[:, r, i, :, :], xt[rows, m % 2, grp, :],
                                                 dm[rows, grp, n0:n0 + 8, :], start=True, stop=True)
                                if i == 1:
                                    last.then_inc(s_dps, 1)

                    def weigh_bc(m):
                        if m == 0:
                            pe.wait_ge(s_dm, ch * 3 + 3 + C_DM)
                        else:
                            pe.wait_ge(s_skp, ch * MD + m)
                        pe.wait_ge(s_slot[m % 2], ch * 192 + 48 * (m // 2) + 48)
                        pe.matmul(ps_m[:, :], w[0:NS, m % 2, W_INVT:W_INVT + P], bc[:, :], start=True, stop=True)\
                            .then_inc(s_bcm, 1)

                    def sum_state(s):
                        m, n = s // NS, s % NS
                        if n == 0 and m >= 2:
                            pe.wait_ge(s_fin, ch * MD + m - 1 + C_FIN)
                        pe.wait_ge(s_q, ch * STEPS + s + 1 + C_Q)
                        pe.matmul(ps_y[:, m % 2, :], w[:, m % 2, n * P:(n + 1) * P], q[:, s % QB, :],
                                  start=(n == 0), stop=(n == NS - 1)).then_inc(s_n, 1)

                    pe.wait_ge(s_xpl, ch * 64 + 64)
                    pe.wait_ge(s_oe, ch * SUB + C_OE)
                    pe.sem_inc(s_pass, 1)
                    for i in range(GRP):
                        last = pe.transpose(ps_m[:, i * NX:(i + 1) * NX],
                                            xpd[:, i * P:(i + 1) * P],
                                            ident[0:NX, 0:NX])
                    last.then_inc(s_bt, 1)
                    turn(0, 0)
                    turn(0, 1)
                    for pair in range(4):
                        if pair % 2 == 0:
                            pe.wait_ge(s_dm, ch * 3 + pair // 2 + 1 + C_DM)
                        make_d(0, pair)
                    weigh_bc(0)
                    for m in range(MD):
                        for n in range(NS):
                            s = m * NS + n
                            half = 2 * m + n // 8 + 1
                            if n % 2 == 0 and half < 2 * MD:
                                make_d(half, (n % 8) // 2)
                            if m + 1 < MD and n in (1, 4):
                                turn(m + 1, n // 4)
                            if m + 1 < MD and n == 13:
                                weigh_bc(m + 1)
                            if s >= LAG:
                                sum_state(s - LAG)
                    for s in range(STEPS - LAG, STEPS):
                        sum_state(s)
                    for i in range(SUB):
                        if i == 0:
                            pe.wait_ge(s_fin, ch * MD + MD + C_FIN)
                        if i >= 2:
                            pe.wait_ge(s_oe, ch * SUB + i - 1 + C_OE)
                        o = ps_m if i % 2 == 0 else ps_x
                        for m in range(MD):
                            last = pe.matmul(o[:, :], y[:, m, i * P:(i + 1) * P], w_out[:, m, :],
                                             start=(m == 0), stop=(m == MD - 1))
                        last.then_inc(s_o, 1)

            @block.vector
            def _(dve):
                must_clip = dve.value_load(clips[0:1, 0:1], min_val=0, max_val=1)
                dve.memset(fac[:, :, 1], -1.0).then_inc(s_slow, 1)
                with dve.Fori(0, BATCH) as b:
                    dve.memset(carry[:, :, :], 0.0).then_inc(s_car, 1)
                    with dve.Fori(0, NCH) as k:
                        ch = b * NCH + k

                        def add_skip(m):
                            dve.wait_ge(s_bcm, ch * MD + m + 1)
                            dve.wait_ge(s_xsl[m % XB], x_loads(ch, m))
                            dve.wait_ge(s_slot[m % 2], ch * 192 + 48 * (m // 2) + 48)
                            dve.scalar_tensor_tensor(skip[:, m % 2, :], ps_m[:, :], w[:, m % 2, W_D:W_D + 1],
                                                     xs[:, m % XB, 1:CH + 1], ALU.add, ALU.mult).then_inc(s_skp, 1)

                        def finish(m):
                            dve.wait_ge(s_n, ch * STEPS + NS * (m + 1))
                            dve.wait_ge(s_skp, ch * MD + m + 1)
                            dve.tensor_tensor(y[:, m, :], ps_y[:, m % 2, :], skip[:, m % 2, :], ALU.add)\
                                .then_inc(s_half, 1)
                            dve.wait_ge(s_half, ch * MD + m + 1)
                            dve.tensor_tensor(y[:, m, :], y[:, m, :], zs[:, m % 2, :], ALU.mult).then_inc(s_fin, 1)

                        def keep(m, n, slot):
                            dve.tensor_copy(carry[:, m, bass.ds(n, 4)], g[:, slot:slot + 4, CH - 1]).then_inc(s_car, 1)

                        def clipped_step(m, n, i, s):
                            at = s * 7 + ch * MD + m + 2

                            def link(ins, j):
                                ins.then_inc(s_slow, 1)
                                dve.wait_ge(s_slow, at + j + 1)
                            free = g[:, i, :]
                            a, d = ps_a[:, i % 2, :], dd[:, bass.ds(n, 1), :].rearrange("p o t -> p (o t)")
                            lim_n = w[:, m % 2, bass.ds(W_LIM + n, 1)]
                            link(dve.tensor_tensor_scan(neg_u[:, :], d, d, neg_u0[:, bass.ds(n, 1)], ALU.add, ALU.bypass), 0)
                            link(dve.tensor_tensor_scan(free, d, a, carry[:, m, bass.ds(n, 1)], ALU.add, ALU.mult), 1)
                            link(dve.tensor_tensor(neg_u[:, :], free, neg_u[:, :], ALU.subtract), 2)
                            dve.tensor_scalar(lim[:, :, 0], neg_u[:, :], -1.0, lim_n, ALU.mult, ALU.add).then_inc(s_slow, 1)
                            dve.tensor_scalar(lim[:, :, 1], neg_u[:, :], lim_n, None, ALU.add).then_inc(s_slow, 1)
                            link(dve.tensor_scalar(fac[:, :, 0], a, -1.0, None, ALU.mult), 5)
                            link(dve.tensor_tensor_scan(lim[:, :, :].rearrange("p t o -> p (t o)"),
                                                        fac[:, :, :].rearrange("p t o -> p (t o)"),
                                                        lim[:, :, :].rearrange("p t o -> p (t o)"),
                                                        0.0, ALU.mult, ALU.min), 6)
                            dve.tensor_tensor(g[:, i, :], free, lim[:, :, 1], ALU.subtract).then_inc(s_g, 1)

                        dve.wait_ge(s_bt, ch + 1)
                        for h in range(2):
                            dve.tensor_tensor(dm[:, 4 * h:4 * h + 4, :, :], bcast(mask_d[:, 0:1], [(0, 4), (0, NS), (1, 32)]),
                                              bcast(ps_m[:, 4 * h * NX + 1:4 * h * NX + 2], [(NX, 4), (1, NS), (0, 32)]),
                                              ALU.mult).then_inc(s_dm, 1)
                        dve.wait_ge(s_xpl, ch * 64 + 64)
                        dve.tensor_tensor(bc[:, :], b_r[:, :], c_r[:, :], ALU.mult).then_inc(s_dm, 1)
                        dve.wait_ge(s_car, ch * (STEPS // 4) + b + 1)
                        dve.sem_inc(s_pass, 1)
                        for m in range(MD):
                            with dve.If(must_clip > 0):
                                if m == 0:
                                    dve.wait_ge(s_ba, ch * 16 + 16)
                                add_skip(m)
                                dve.tensor_scalar(neg_u0[:, :], b_ahead[:, :], xs[:, m % XB, 0:1], -1.0, ALU.mult, ALU.mult)\
                                    .then_inc(s_slow, 1)
                                for h in range(2):
                                    dve.wait_ge(s_dd, ch * STEPS + 8 * (2 * m + h + 1))
                                    dve.sem_inc(s_pass, 1)
                                    with dve.Fori(0, 2) as j:
                                        for i in range(4):
                                            n = j * 4 + (8 * h + i)
                                            s = ch * STEPS + m * NS + n
                                            dve.wait_ge(s_slow, s * 7 + ch * MD + m + 2)
                                            dve.wait_ge(s_a, s + 1)
                                            dve.wait_ge(s_q, s + 1 - GB + C_Q)
                                            clipped_step(m, n, i, s + 0)
                                        dve.wait_ge(s_g, ch * STEPS + m * NS + j * 4 + 8 * h + 4)
                                        dve.sem_inc(s_pass, 1)
                                        keep(m, j * 4 + 8 * h, 0)
                                    if h == 0 and m > 0:
                                        finish(m - 1)
                            with dve.Else():
                                for n in range(NS):
                                    s = m * NS + n
                                    if n % 8 == 0:
                                        dve.wait_ge(s_dd, ch * STEPS + s + 8)
                                    dve.wait_ge(s_a, ch * STEPS + s + 1)
                                    if n % 4 == 0 and s > 0:
                                        dve.wait_ge(s_car, ch * (STEPS // 4) + b + 1 + s // 4)
                                    if s >= GB:
                                        dve.wait_ge(s_q, ch * STEPS + s - GB + 1 + C_Q)
                                    dve.tensor_tensor_scan(g[:, s % GB, :], dd[:, n, :], ps_a[:, n % 2, :],
                                                           carry[:, m, n:n + 1], ALU.add, ALU.mult).then_inc(s_g, 1)
                                    if n == 3:
                                        add_skip(m)
                                    if n == 5 and m > 0:
                                        finish(m - 1)
                                    if n % 4 == 3:
                                        dve.wait_ge(s_g, ch * STEPS + s + 1)
                                        keep(m, n - 3, 0)
                        finish(MD - 1)
                        dve.wait_ge(s_res, ch * 16 + 16)
                        for i in range(SUB):
                            dve.wait_ge(s_o, ch * SUB + i + 1)
                            o = ps_m if i % 2 == 0 else ps_x
                            dve.tensor_tensor(res[:, i, :], o[:, :], res[:, i, :], ALU.add).then_inc(s_oe, 1)


def ffn(nc, sb, sem, t_in, ident, minus_half, x1_d, out):
    with ExitStack() as c:
        w_sh, w_ex = sb("w_sh", [P, KD, DM], c=c), sb("w_ex", [P, KD, DM], c=c)
        w_g = sb("w_g", [P, KD, GATES], c=c)
        bias = sb("bias", [P, DM], c=c)
        x = sb("x_c", [P, 2, SUB, DM], c=c)
        stats, mv = sb("stats_c", [P, SUB, 6], c=c), sb("mv_c", [P, SUB, 2], c=c)
        var, rstd = sb("var_c", [P, SUB], c=c), sb("rstd_c", [P, SUB], c=c)
        xn = sb("xn_c", [P, SUB, DM], c=c)
        xnt = sb("xnt_c", [P, SUB, KD, P], c=c)
        xb = sb("xb_c", [P, SUB, DM], c=c)
        o = sb("o_c", [P, 2, SUB, DM], c=c)
        gmax, gate = sb("gmax", [P, SUB], c=c), sb("gate", [P, SUB, 8], c=c)
        z, rz = sb("z", [P, SUB], c=c), sb("rz", [P, SUB], c=c)
        top = sb("top", [P, SUB, 8], c=c)
        den, rden = sb("den", [P, SUB], c=c), sb("rden", [P, SUB], c=c)
        pick, wsum = sb("pick", [P, SUB, TOPK], c=c), sb("wsum", [P, SUB], c=c)
        ps_t = c.enter_context(nc.psum_tensor("ps_t_c", [P, 2, DM], F32))
        ps_s = c.enter_context(nc.psum_tensor("ps_s", [P, 2, DM], F32))
        ps_e = c.enter_context(nc.psum_tensor("ps_e", [P, 2, DM], F32))
        ps_g = c.enter_context(nc.psum_tensor("ps_g", [P, DM], F32))
        S = lambda n: sem("c_" + n, c)
        s_pass = S("pass")
        s_wt, s_st, s_pow, s_xn, s_xb = S("weights"), S("stats"), S("pow"), S("xn"), S("xb")
        s_x, s_out = [S("x0"), S("x1")], [S("out0"), S("out1")]
        s_one, s_tr, s_te, s_g, s_s, s_e = S("one"), S("tr"), S("te"), S("g"), S("s"), S("e")
        s_gx, s_ge, s_w, s_sx, s_fin = S("gx"), S("ge"), S("w"), S("sx"), S("fin")
        ITER = TOKENS // (2 * CH)
        DV = 2 * SUB + 9

        with nc.Block() as block:
            @block.sync
            def _(sp):
                for dst, src in ((w_sh[:, :, :], t_in["W_sharedT"].rearrange("(k p) n -> p k n", p=P)),
                                 (w_ex[:, :, :], t_in["W_expertT"].rearrange("(k p) n -> p k n", p=P)),
                                 (w_g[:, :, :], t_in["W_gate"].rearrange("(k p) n -> p k n", p=P)),
                                 (bias[:, :], t_in["bias"].partition_broadcast(P))):
                    sp.dma_start(dst, src).then_inc(s_wt, 16)
                with sp.Fori(0, ITER) as it:
                    for e in range(2):
                        sp.wait_ge(s_fin, it * (2 * SUB) + e * SUB + SUB)
                        sp.dma_start(x[:, e, :, :], x1_d[bass.ds(it * (2 * CH) + e * CH, CH), :]
                                     .rearrange("(s p) d -> p s d", p=P)).then_inc(s_x[e], 16)

            @block.gpsimd
            def _(pool):
                pool.sem_inc(s_fin, 2 * SUB)
                pool.sem_inc(s_sx, SUB)
                for e in range(2):
                    pool.sem_inc(s_out[e], 1)
                pool.memset(gate[:, :, :], -1.0).then_inc(s_ge, 1)
                pool.wait_ge(s_wt, 64)
                with pool.Fori(0, ITER) as it:
                    for e in range(2):
                        pool.wait_ge(s_st, it * 2 + e + 1)
                        pool.tensor_tensor(rstd[:, :], var[:, :], minus_half[:, :], ALU.pow).then_inc(s_pow, 1)
                        for i in range(SUB):
                            pool.wait_ge(s_fin, it * (2 * SUB) + e * SUB + i + 1 + SUB)
                            pool.tensor_tensor(xb[:, i, :], x[:, e, i, :], bias[:, :], ALU.add).then_inc(s_xb, 1)

            @block.scalar
            def _(act):
                with act.Fori(0, ITER) as it:
                    for e in range(2):
                        ch = it * 2 + e
                        for i in range(SUB):
                            act.wait_ge(s_tr, ch * SUB + i + 1)
                            act.activation(xnt[:, i, :, :], ps_t[:, i % 2, :], ACT.Copy).then_inc(s_te, 1)
                        act.wait_ge(s_gx, ch * 1 + 1)
                        act.activation(gate[:, :, 0:GATES], gate[:, :, 0:GATES], ACT.Exp).then_inc(s_ge, 1)
                        act.wait_ge(s_fin, ch * SUB + SUB + 2 * SUB)
                        act.dma_start(out[bass.ts(ch, CH), :].rearrange("(s p) d -> p s d", p=P), o[:, e, :, :])\
                            .then_inc(s_out[e], 16)
                for e in range(2):
                    act.wait_ge(s_out[e], ITER * 16 + 1)

            @block.tensor
            def _(pe):
                pe.wait_ge(s_wt, 64)
                with pe.Fori(0, ITER) as it:
                    for e in range(2):
                        ch = it * 2 + e
                        for i in range(SUB):
                            pe.wait_ge(s_xn, ch * SUB + i + 1)
                            if i >= 2:
                                pe.wait_ge(s_te, ch * SUB + i - 1)
                            for q in range(KD):
                                last = pe.transpose(ps_t[:, i % 2, q * P:(q + 1) * P], xn[:, i, q * P:(q + 1) * P],
                                                    ident[:, :])
                            last.then_inc(s_tr, 1)
                        for i in range(SUB):
                            pe.wait_ge(s_te, ch * SUB + i + 1)
                            for q in range(KD):
                                last = pe.matmul(ps_g[:, i * 8:i * 8 + GATES], xnt[:, i, q, :], w_g[:, q, :],
                                                 start=(q == 0), stop=(q == KD - 1))
                        last.then_inc(s_g, 1)
                        for i in range(SUB):
                            pe.wait_ge(s_sx, ch * SUB + i - 1 + SUB)
                            for q in range(KD):
                                last = pe.matmul(ps_s[:, i % 2, :], xnt[:, i, q, :], w_sh[:, q, :],
                                                 start=(q == 0), stop=(q == KD - 1))
                            last.then_inc(s_s, 1)
                            pe.wait_ge(s_fin, ch * SUB + i - 1 + 2 * SUB)
                            for q in range(KD):
                                last = pe.matmul(ps_e[:, i % 2, :], xnt[:, i, q, :], w_ex[:, q, :],
                                                 start=(q == 0), stop=(q == KD - 1))
                            last.then_inc(s_e, 1)

            @block.vector
            def _(dve):
                dve.wait_ge(s_ge, 1)
                with dve.Fori(0, ITER) as it:
                    for e in range(2):
                        ch = it * 2 + e
                        at = [0]

                        def step(ins, wait=True):
                            at[0] += 1
                            ins.then_inc(s_one, 1)
                            if wait:
                                dve.wait_ge(s_one, ch * DV + at[0])
                                dve.sem_inc(s_pass, 1)
                        dve.wait_ge(s_x[e], it * 16 + 16)
                        for i in range(SUB):
                            step(dve.bn_stats(stats[:, i, :], x[:, e, i, :]), i == SUB - 1)
                        for i in range(SUB):
                            step(dve.bn_aggr(mv[:, i, :], stats[:, i, :]), i == SUB - 1)
                        dve.tensor_scalar(var[:, :], mv[:, :, 1], EPS, None, ALU.add).then_inc(s_st, 1)
                        dve.wait_ge(s_pow, ch + 1)
                        for i in range(SUB):
                            dve.tensor_scalar(xn[:, i, :], x[:, e, i, :], mv[:, i, 0:1], rstd[:, i:i + 1],
                                              ALU.subtract, ALU.mult).then_inc(s_xn, 1)
                        dve.wait_ge(s_g, ch + 1)
                        logits = bcast(ps_g[:, 0:1], [(8, SUB), (1, GATES)])
                        step(dve.tensor_reduce(gmax[:, :], logits, AX.X, ALU.max))
                        dve.tensor_tensor(gate[:, :, 0:GATES], logits, bcast(gmax[:, 0:1], [(1, SUB), (0, GATES)]),
                                          ALU.subtract).then_inc(s_gx, 1)
                        dve.wait_ge(s_ge, ch + 2)
                        step(dve.tensor_reduce(z[:, :], gate[:, :, 0:GATES], AX.X, ALU.add))
                        step(dve.reciprocal(rz[:, :], z[:, :]))
                        step(dve.tensor_tensor(gate[:, :, 0:GATES], gate[:, :, 0:GATES],
                                               bcast(rz[:, 0:1], [(1, SUB), (0, GATES)]), ALU.mult))
                        dve.sem_inc(s_pass, 1)
                        for i in range(SUB):
                            last = dve.max(top[:, i, :], gate[:, i, :])
                        step(last)
                        step(dve.tensor_reduce(den[:, :], top[:, :, 0:TOPK], AX.X, ALU.add))
                        step(dve.reciprocal(rden[:, :], den[:, :]))
                        step(dve.tensor_tensor(pick[:, :, :], top[:, :, 0:TOPK],
                                               bcast(rden[:, 0:1], [(1, SUB), (0, TOPK)]), ALU.mult))
                        step(dve.tensor_reduce(wsum[:, :], pick[:, :, :], AX.X, ALU.add))
                        assert at[0] == DV
                        dve.wait_ge(s_out[e], it * 16 + 1)
                        for i in range(SUB):
                            dve.wait_ge(s_xb, ch * SUB + i + 1)
                            dve.wait_ge(s_s, ch * SUB + i + 1)
                            dve.tensor_tensor(xb[:, i, :], ps_s[:, i % 2, :], xb[:, i, :], ALU.add).then_inc(s_sx, 1)
                            dve.wait_ge(s_sx, ch * SUB + i + 1 + SUB)
                            dve.wait_ge(s_e, ch * SUB + i + 1)
                            dve.scalar_tensor_tensor(o[:, e, i, :], ps_e[:, i % 2, :], wsum[:, i:i + 1], xb[:, i, :],
                                                     ALU.mult, ALU.add).then_inc(s_fin, 1)


def kernel(**inputs):
    import numpy as np
    import concourse.bacc as bacc
    from concourse.bass_utils import run_bass_kernel_spmd

    a = {k[3:].split("_", 1)[1]: np.asarray(v) for k, v in inputs.items()}
    def columns(v):
        return v.reshape(-1, P).T

    laid = {
        "x": a["x"].reshape(TOKENS, DM), "ln_gamma": columns(a["ln_gamma"]), "ln_beta": columns(a["ln_beta"]),
        "W_inT": a["W_in"].T, "conv_w": a["conv_w"].reshape(DI, TAPS), "conv_b": columns(a["conv_b"]),
        "A_log": a["A_log"], "D_param": columns(a["D_param"]), "W_xprojT": a["W_xproj"].T, "W_dtT": a["W_dt"].T,
        "b_dt": columns(a["b_dt"]), "W_outT": a["W_out"].T, "W_sharedT": a["W_shared"].T, "W_expertT": a["W_expert"].T,
        "W_gate": a["W_gate"], "bias": a["bias"],
    }
    nc = bacc.Bacc("TRN2", target_bir_lowering=False, num_devices=1)
    arrays, t_in = {}, {}
    for name, v in laid.items():
        arrays["in_" + name] = np.ascontiguousarray(v)
        t_in[name] = nc.dram_tensor("in_" + name, v.shape, mybir.dt.from_np(v.dtype), kind="ExternalInput").ap()
    out = nc.dram_tensor("out", (TOKENS, DM), F32, kind="ExternalOutput").ap()
    build(nc, t_in, out)
    r = run_bass_kernel_spmd(nc, [arrays], core_ids=[0])
    return r.results[0]["out"].reshape(BATCH, LEN, DM)
```

```python
import concourse.bass as bass
from concourse import mybir
from contextlib import ExitStack

P = 128
BATCH, LEN, DM = 2, 4096, 512
DI, NS, TAPS, NX = 1024, 16, 4, 33
TOKENS = BATCH * LEN
CH = 512
NCH = LEN // CH
KD = DM // P
MD = DI // P
SUB = CH // P
GRP = CH // 64
GATES, TOPK = 7, 2
EPS = 1e-5
PAD = LEN + 1

W_DIAG, W_INVT, W_A, W_D, W_LIM = 0, NS * P, NS * P + P, NS * P + P + NS, NS * P + P + NS + 1
W_INV = W_LIM + NS
W_COLS = W_INV + NS

F32 = mybir.dt.float32
I32 = mybir.dt.int32
F32R = mybir.dt.float32r
ALU = mybir.AluOpType
ACT = mybir.ActivationFunctionType
AX = mybir.AxisListType


def bcast(ap, dims):
    return bass.AP(tensor=ap.tensor, offset=ap.offset, ap=[tuple(ap.ap[0])] + dims)


def build(nc, t_in, out):
    with ExitStack() as ctx:
        def sb(name, shape, dt=F32, c=None):
            return (c or ctx).enter_context(nc.sbuf_tensor(name, shape, dt))

        def sem(name, c=None):
            return (c or ctx).enter_context(nc.semaphore(name))

        xs_d = nc.dram_tensor("xs_d", [BATCH, MD, P, PAD], F32).ap()
        dt_d = nc.dram_tensor("dt_d", [BATCH, MD, P, LEN], F32).ap()
        zs_d = nc.dram_tensor("zs_d", [BATCH, MD, P, LEN], F32).ap()
        xp_d = nc.dram_tensor("xp_d", [BATCH, NX, PAD], F32).ap()
        w_d = nc.dram_tensor("w_d", [MD, P, W_COLS], F32).ap()
        y_d = nc.dram_tensor("y_d", [BATCH, MD, P, LEN], F32).ap()

        ident = sb("ident", [P, P])
        mask_d = sb("mask_d", [P, 32])
        minus_half = sb("minus_half", [P, SUB])
        clips = sb("clips", [1, 1], I32)
        with ExitStack() as early:
            ones = sb("ones", [P, P], c=early)
            margin = sb("margin", [P, MD, NS], c=early)
            within = sb("within", [P, MD, NS], c=early)
            setup(nc, sb, sem, t_in, ident, ones, mask_d, minus_half, margin, within, xs_d, xp_d, w_d)
            front(nc, sb, sem, t_in, ident, ones, minus_half, margin, within, clips, xs_d, dt_d, zs_d, xp_d)
        scan(nc, sb, sem, ident, mask_d, clips, xs_d, dt_d, zs_d, xp_d, w_d, y_d)
        ffn(nc, sb, sem, t_in, ident, minus_half, y_d, out)


def setup(nc, sb, sem, t_in, ident, ones, mask_d, minus_half, margin, within, xs_d, xp_d, w_d):
    with ExitStack() as c:
        zeros = sb("zeros", [P, 16], c=c)
        a_log = sb("a_log", [P, MD, NS], c=c)
        ea = sb("ea", [P, MD, NS], c=c)
        ap_ = sb("ap_", [P, MD, NS], c=c)
        an = sb("an", [P, MD, NS], c=c)
        inv = sb("inv", [P, MD, NS], c=c)
        d_par = sb("d_par", [P, MD], c=c)
        w = sb("w", [P, 2, W_COLS], c=c)
        ps = c.enter_context(nc.psum_tensor("ps_setup", [NS, MD, P], F32))
        s_in, s_pool, s_exp, s_dve = sem("su_in", c), sem("su_pool", c), sem("su_exp", c), sem("su_dve", c)
        s_tr, s_w, s_zero = sem("su_tr", c), sem("su_w", c), sem("su_zero", c)
        s_wo = [sem(f"su_wo{i}", c) for i in range(2)]

        with nc.Block() as block:
            @block.sync
            def _(sp):
                sp.dma_start(a_log[:, :, :], t_in["A_log"].rearrange("(m p) n -> p m n", p=P)).then_inc(s_in, 16)
                sp.dma_start(d_par[:, :], t_in["D_param"]).then_inc(s_in, 16)
                sp.wait_ge(s_pool, 1)
                for b in range(BATCH):
                    sp.dma_start(xs_d[b, :, :, 0:1].rearrange("m p o -> p m o"), zeros[:, 0:MD],
                                 allow_slow_non_contiguous=True).then_inc(s_zero, 16)
                    sp.dma_start(xp_d[b, :, 0:1], zeros[0:NX, 0:1],
                                 allow_slow_non_contiguous=True).then_inc(s_zero, 16)
                for m in range(MD):
                    sp.wait_ge(s_w, m + 1)
                    sp.dma_start(w_d[m, :, :], w[:, m % 2, :]).then_inc(s_wo[m % 2], 16)
                for i in range(2):
                    sp.wait_ge(s_wo[i], 16 * MD // 2)
                sp.wait_ge(s_zero, 16 * 2 * BATCH)

            @block.gpsimd
            def _(pool):
                pool.memset(zeros[:, :], 0.0).then_inc(s_pool, 1)
                pool.memset(ident[:, :], 0.0).then_inc(s_pool, 1)
                pool.memset(mask_d[:, :], 0.0).then_inc(s_pool, 1)
                pool.memset(ones[:, :], 1.0).then_inc(s_pool, 1)
                pool.memset(minus_half[:, :], -0.5).then_inc(s_pool, 1)
                pool.memset(within[:, :, :], 1.0).then_inc(s_pool, 1)
                pool.wait_ge(s_pool, 6)
                pool.affine_select(out=ident[:, :], in_=ident[:, :], compare_op=ALU.not_equal, fill=1.0,
                                   base=0, pattern=[[-1, P]], channel_multiplier=1).then_inc(s_pool, 1)
                for k in range(4):
                    pool.affine_select(out=mask_d[:, :], in_=mask_d[:, :], compare_op=ALU.not_equal,
                                       fill=1.0 if k % 2 == 0 else -1.0, base=-32 * k, pattern=[[-1, 32]],
                                       channel_multiplier=1).then_inc(s_pool, 1)
                    pool.wait_ge(s_pool, 8 + k)

            @block.scalar
            def _(act):
                act.wait_ge(s_in, 32)
                act.activation(ea[:, :, :], a_log[:, :, :], ACT.Exp).then_inc(s_exp, 1)

            @block.tensor
            def _(pe):
                pe.wait_ge(s_pool, 7)
                pe.wait_ge(s_dve, 4)
                for m in range(MD):
                    last = pe.transpose(ps[:, m, :], inv[:, m, :], ident[:, :])
                last.then_inc(s_tr, 1)

            @block.vector
            def _(dve):
                done = [0]

                def step(ins):
                    done[0] += 1
                    ins.then_inc(s_dve, 1)
                    dve.wait_ge(s_dve, done[0])
                dve.wait_ge(s_exp, 1)
                step(dve.tensor_scalar(ap_[:, :, :], ea[:, :, :], -1.0, 1e-8, ALU.mult, ALU.add))
                step(dve.tensor_scalar(an[:, :, :], ap_[:, :, :], -1.0, None, ALU.mult))
                step(dve.tensor_tensor(an[:, :, :], an[:, :, :], ap_[:, :, :], ALU.max))
                step(dve.reciprocal(inv[:, :, :], ap_[:, :, :]))
                step(dve.tensor_scalar(margin[:, :, :], an[:, :, :], 9.9, None, ALU.mult))
                step(dve.memset(w[:, :, :], 0.0))
                dve.wait_ge(s_pool, 7)
                dve.wait_ge(s_tr, 1)
                for m in range(MD):
                    e = m % 2
                    if m >= 2:
                        dve.wait_ge(s_wo[e], 16 * (m // 2))
                    step(dve.tensor_tensor(w[:, e, W_DIAG:W_DIAG + NS * P].rearrange("p (n k) -> p n k", n=NS),
                                           bcast(ident[:, :], [(0, NS), (1, P)]),
                                           bcast(inv[:, m, :], [(1, NS), (0, P)]), ALU.mult))
                    step(dve.tensor_copy(w[0:NS, e, W_INVT:W_INVT + P], ps[:, m, :]))
                    step(dve.tensor_scalar(w[:, e, W_A:W_A + NS], ea[:, m, :], -1.0, None, ALU.mult))
                    step(dve.tensor_copy(w[:, e, W_D:W_D + 1], d_par[:, m:m + 1]))
                    step(dve.tensor_scalar(w[:, e, W_LIM:W_LIM + NS], an[:, m, :], 10.0, None, ALU.mult))
                    step(dve.tensor_copy(w[:, e, W_INV:W_INV + NS], inv[:, m, :]))
                    dve.sem_inc(s_w, 1)


def front(nc, sb, sem, t_in, ident, ones, minus_half, margin, within, clips, xs_d, dt_d, zs_d, xp_d):
    HALO = TAPS - 1
    RING = 4
    with ExitStack() as c:
        w_hi, w_lo = sb("w_hi", [P, KD, 2 * DI], F32R, c), sb("w_lo", [P, KD, 2 * DI], F32R, c)
        w_xp = sb("w_xp", [P, MD, NX], c=c)
        w_dt = sb("w_dt", [NX, DI], c=c)
        gamma, beta = sb("gamma", [P, KD], c=c), sb("beta", [P, KD], c=c)
        taps, cbias, bdt = sb("taps", [P, MD, TAPS], c=c), sb("cbias", [P, MD], c=c), sb("bdt", [P, MD], c=c)
        bdt1 = sb("bdt1", [P, MD], c=c)
        x = sb("x_f", [P, SUB, DM], c=c)
        stats, mv = sb("stats_f", [P, SUB, 6], c=c), sb("mv_f", [P, SUB, 2], c=c)
        spread, rstd = sb("spread_f", [P, SUB], c=c), sb("rstd_f", [P, SUB], c=c)
        xn = sb("xn_f", [P, SUB, DM], c=c)
        xnt = sb("xnt_f", [P, KD, CH], c=c)
        xnt_hi, xnt_lo = sb("xnt_hi", [P, KD, CH], F32R, c), sb("xnt_lo", [P, KD, CH], F32R, c)
        xz = sb("xz", [P, MD, HALO + CH], c=c)
        conv = sb("conv", [P, 2, CH], c=c)
        zs = sb("zs_f", [P, RING, CH], c=c)
        xs = sb("xs_f", [P, MD, CH], c=c)
        xp = sb("xp_f", [NX, CH], c=c)
        v = sb("v_f", [P, MD, CH], c=c)
        lg = sb("lg_f", [P, MD, CH], c=c)
        xmax, bmax = sb("xmax", [P, MD], c=c), sb("bmax", [NX, 1], c=c)
        bdiag = sb("bdiag", [NX, NX], c=c)
        umax, inside = sb("umax", [P, MD, NS], c=c), sb("inside", [P, MD, NS], c=c)
        inside1 = sb("inside1", [P, 1], c=c)
        ps_t = c.enter_context(nc.psum_tensor("ps_t_f", [P, 2, CH], F32))
        ps_r = c.enter_context(nc.psum_tensor("ps_r_f", [P, RING, CH], F32))
        ps_xp = c.enter_context(nc.psum_tensor("ps_xp", [P, CH], F32))
        ps_b = c.enter_context(nc.psum_tensor("ps_b", [P, CH], F32))

        S = lambda n: sem("f_" + n, c)
        s_wt, s_x, s_one = S("weights"), S("x"), S("one")
        s_st, s_pow, s_xn, s_tr, s_te = S("stats"), S("pow"), S("xn"), S("tr"), S("te")
        s_mm, s_xe, s_z, s_cv, s_xs = S("mm"), S("xe"), S("z"), S("cv"), S("xs")
        s_halo, s_xm, s_xpm, s_xpe, s_xpo = S("halo"), S("xm"), S("xpm"), S("xpe"), S("xpo")
        s_v, s_abs, s_ex, s_ln = S("v"), S("abs"), S("ex"), S("ln")
        s_dt, s_dto, s_xso, s_hi, s_lo, s_xl, s_b1 = S("dt"), S("dto"), S("xso"), S("hi"), S("lo"), S("xl"), S("b1")
        s_zo = [S(f"zo{i}") for i in range(RING)]
        s_pass, s_bd, s_bb, s_in, s_fl = S("pass"), S("bd"), S("bb"), S("in"), S("flag")

        with nc.Block() as block:
            @block.sync
            def _(sp):
                for stage, at in ((v, 0), (lg, KD // 2)):
                    sp.dma_start(stage[:, :, :].rearrange("p m t -> p (m t)").rearrange("p (k n) -> p k n", n=2 * DI),
                                 t_in["W_inT"][at * P:(at + KD // 2) * P, :].rearrange("(k p) n -> p k n", p=P))\
                        .then_inc(s_wt, 16)
                for dst, src in ((w_xp[:, :, :], t_in["W_xprojT"].rearrange("(k p) n -> p k n", p=P)),
                                 (w_dt[:, :], t_in["W_dtT"]),
                                 (gamma[:, :], t_in["ln_gamma"]),
                                 (beta[:, :], t_in["ln_beta"]),
                                 (taps[:, :, :], t_in["conv_w"].rearrange("(m p) k -> p m k", p=P)),
                                 (cbias[:, :], t_in["conv_b"]),
                                 (bdt[:, :], t_in["b_dt"])):
                    sp.dma_start(dst, src).then_inc(s_wt, 16)
                sp.dma_start(x[:, :, :], t_in["x"][0:CH, :].rearrange("(s p) d -> p s d", p=P)).then_inc(s_x, 16)
                with sp.Fori(0, BATCH) as b:
                    with sp.Fori(0, NCH) as k:
                        ch = b * NCH + k
                        after = (ch + 1) % (BATCH * NCH)
                        sp.wait_ge(s_xn, ch * SUB + SUB)
                        sp.dma_start(x[:, :, :], t_in["x"][bass.ts(after, CH), :].rearrange("(s p) d -> p s d", p=P))\
                            .then_inc(s_x, 16)
                        sp.wait_ge(s_xpe, ch + 1)
                        sp.dma_start(xp_d[b, :, bass.ds(k * CH + 1, CH)], xp[:, :]).then_inc(s_xpo, 16)
                        for h in range(2):
                            m0, m1 = h * MD // 2, (h + 1) * MD // 2
                            sp.wait_ge(s_dt, ch * 2 + h + 2)
                            sp.dma_start(dt_d[b, m0:m1, :, bass.ts(k, CH)].rearrange("m p t -> p m t"),
                                         lg[:, m0:m1, :]).then_inc(s_dto, 16)
                sp.wait_ge(s_x, 16 * (BATCH * NCH + 1))
                sp.wait_ge(s_xpo, BATCH * NCH * 16 + 1)
                sp.wait_ge(s_dto, BATCH * NCH * 32 + 1)

            @block.gpsimd
            def _(pool):
                pool.sem_inc(s_xpo, 1)
                pool.sem_inc(s_dto, 1)
                pool.sem_inc(s_xso, 1)
                pool.sem_inc(s_dt, 1)
                pool.sem_inc(s_xm, 1)
                pool.sem_inc(s_v, RING)
                for i in range(RING):
                    pool.sem_inc(s_zo[i], 1)
                def inverse_spread(n):
                    pool.wait_ge(s_st, n)
                    pool.tensor_tensor(rstd[:, :], spread[:, :], minus_half[:, :], ALU.pow).then_inc(s_pow, 1)

                def rest_of_xnt(ch):
                    for q in range(KD):
                        pool.wait_ge(s_te, ch * (2 * KD) + 2 * q + 2)
                        pool.tensor_tensor(xnt_lo[:, q, :], xnt[:, q, :], xnt_hi[:, q, :].bitcast(F32), ALU.subtract)\
                            .then_inc(s_xl, 1)

                inverse_spread(1)
                rest_of_xnt(0)
                with pool.Fori(0, BATCH * NCH) as ch:
                    inverse_spread(ch + 2)
                    rest_of_xnt(ch + 1)
                    for h in range(2):
                        m0, m1 = h * MD // 2, (h + 1) * MD // 2
                        pool.wait_ge(s_ln, ch * 2 + h + 1)
                        pool.wait_ge(s_v, ch * MD + m1 + RING)
                        pool.tensor_tensor(lg[:, m0:m1, :], lg[:, m0:m1, :], v[:, m0:m1, :], ALU.add)\
                            .then_inc(s_dt, 1)

            @block.scalar
            def _(act):
                def scale_xnt(ch, q):
                    act.wait_ge(s_tr, ch * KD + q + 1)
                    for dst in (xnt, xnt_hi):
                        act.activation(dst[:, q, :], ps_t[:, q % 2, :], ACT.Identity,
                                       scale=gamma[:, q:q + 1], bias=beta[:, q:q + 1]).then_inc(s_te, 1)

                act.wait_ge(s_wt, 9 * 16)
                for j, stage in enumerate((v, lg)):
                    act.activation(w_hi[:, 2 * j:2 * j + 2, :].rearrange("p k n -> p (k n)"),
                                   stage[:, :, :].rearrange("p m t -> p (m t)"), ACT.Copy).then_inc(s_hi, 1)
                for q in range(KD):
                    scale_xnt(0, q)
                act.wait_ge(s_lo, 2)
                with act.Fori(0, BATCH) as b:
                    with act.Fori(0, NCH) as k:
                        ch = b * NCH + k
                        act.wait_ge(s_halo, ch + b + 1)
                        for m in range(MD):
                            act.wait_ge(s_mm, ch * 24 + m + 1)
                            act.activation(xz[:, m, HALO:HALO + CH], ps_r[:, m % RING, :], ACT.Copy).then_inc(s_xe, 1)
                        act.wait_ge(s_xm, ch + 1)
                        act.wait_ge(s_xso, ch * (16 * MD) + 1)
                        for m in range(MD):
                            act.wait_ge(s_mm, ch * 24 + MD + m + 1)
                            act.wait_ge(s_zo[m % RING], ch * 32 + (m // RING) * 16 + 1)
                            act.activation(zs[:, m % RING, :], ps_r[:, m % RING, :], ACT.Silu).then_inc(s_z, 1)
                            act.wait_ge(s_z, ch * MD + m + 1)
                            act.dma_start(zs_d[b, m, :, bass.ts(k, CH)], zs[:, m % RING, :]).then_inc(s_zo[m % RING], 16)
                            act.wait_ge(s_cv, ch * 32 + 4 * m + 4)
                            act.activation(xs[:, m, :], conv[:, m % 2, :], ACT.Silu).then_inc(s_xs, 1)
                            act.wait_ge(s_xs, ch * MD + m + 1)
                            act.dma_start(xs_d[b, m, :, bass.ds(k * CH + 1, CH)], xs[:, m, :]).then_inc(s_xso, 16)
                        act.wait_ge(s_xl, ch * KD + KD)
                        act.wait_ge(s_dto, ch * 32 + 1)
                        for m in range(MD):
                            if m % 4 == 0:
                                scale_xnt(ch + 1, m // 2)
                                scale_xnt(ch + 1, m // 2 + 1)
                            act.wait_ge(s_mm, ch * 24 + 2 * MD + m + 1)
                            act.activation(lg[:, m, :], ps_r[:, m % RING, :], ACT.Abs, bias=bdt[:, m:m + 1])\
                                .then_inc(s_abs, 1)
                        for h in range(2):
                            m0, m1 = h * MD // 2, (h + 1) * MD // 2
                            act.wait_ge(s_abs, ch * MD + m1)
                            act.activation(lg[:, m0:m1, :], lg[:, m0:m1, :], ACT.Exp, scale=-1.0).then_inc(s_ex, 1)
                        for h in range(2):
                            m0, m1 = h * MD // 2, (h + 1) * MD // 2
                            act.wait_ge(s_ex, ch * 2 + h + 1)
                            act.activation(lg[:, m0:m1, :], lg[:, m0:m1, :], ACT.Ln, bias=1.0).then_inc(s_ln, 1)
                act.wait_ge(s_xso, BATCH * NCH * MD * 16 + 1)
                for i in range(RING):
                    act.wait_ge(s_zo[i], BATCH * NCH * 32 + 1)

            @block.tensor
            def _(pe):
                def transpose_xn(ch, q):
                    if q >= 2:
                        pe.wait_ge(s_te, ch * (2 * KD) + 2 * (q - 1))
                    for s in range(SUB):
                        if q == 0:
                            pe.wait_ge(s_xn, ch * SUB + s + 1)
                            pe.sem_inc(s_pass, 1)
                        last = pe.transpose(ps_t[:, q % 2, s * P:(s + 1) * P], xn[:, s, q * P:(q + 1) * P], ident[:, :])
                    last.then_inc(s_tr, 1)

                pe.wait_ge(s_wt, 9 * 16)
                for q in range(KD):
                    transpose_xn(0, q)
                pe.wait_ge(s_lo, 2)
                with pe.Fori(0, BATCH * NCH) as ch:
                    for r in range(2 * MD):
                        if r < RING:
                            pe.wait_ge(s_v, ch * MD + r + 1)
                        elif r < RING + MD:
                            pe.wait_ge(s_xe, ch * MD + r - RING + 1)
                        else:
                            pe.wait_ge(s_z, ch * MD + r - RING - MD + 1)
                        for q in range(KD):
                            if r == 0:
                                pe.wait_ge(s_xl, ch * KD + q + 1)
                            cols = slice(r * P, (r + 1) * P)
                            for j, (wp, xp_) in enumerate(((w_hi, xnt_hi), (w_lo, xnt_hi), (w_hi, xnt_lo))):
                                last = pe.matmul(ps_r[:, r % RING, :], wp[:, q, cols], xp_[:, q, :],
                                                 start=(q + j == 0), stop=(q == KD - 1 and j == 2))
                        last.then_inc(s_mm, 1)
                    for m in range(MD):
                        pe.wait_ge(s_xs, ch * MD + m + 1)
                        last = pe.matmul(ps_xp[0:NX, :], w_xp[:, m, :], xs[:, m, :], start=(m == 0), stop=(m == MD - 1))
                    last.then_inc(s_xpm, 1)
                    for m in range(MD):
                        r = 2 * MD + m
                        if m % 4 == 0:
                            transpose_xn(ch + 1, m // 2)
                            transpose_xn(ch + 1, m // 2 + 1)
                        if m == 0:
                            pe.wait_ge(s_xpe, ch + 1)
                        if m < RING:
                            pe.wait_ge(s_z, ch * MD + m + RING + 1)
                        else:
                            pe.wait_ge(s_v, ch * MD + m - RING + 1 + RING)
                        pe.matmul(ps_r[:, r % RING, :], w_dt[:, m * P:(m + 1) * P], xp[:, :], start=True, stop=True)\
                            .then_inc(s_mm, 1)
                    pe.wait_ge(s_bd, ch + 1)
                    pe.matmul(ps_b[:, 0:NX], ones[0:NX, :], bdiag[:, :], start=True, stop=True).then_inc(s_bb, 1)
                pe.wait_ge(s_fl, 1)
                pe.matmul(ps_b[0:1, 0:1], ones[:, 0:1], inside1[:, :], start=True, stop=True).then_inc(s_fl, 1)

            @block.vector
            def _(dve):
                def spread_of(ch):
                    dve.wait_ge(s_x, ch * 16 + 16)
                    for s in range(SUB):
                        dve.bn_stats(stats[:, s, :], x[:, s, :]).then_inc(s_one, 1)
                    for s in range(SUB):
                        dve.wait_ge(s_one, ch * 8 + s + 1)
                        dve.sem_inc(s_pass, 1)
                        dve.bn_aggr(mv[:, s, :], stats[:, s, :]).then_inc(s_one, 1)
                    dve.wait_ge(s_one, ch * 8 + 8)
                    dve.tensor_scalar(spread[:, :], mv[:, :, 1], 1.0 + EPS, EPS * EPS, ALU.mult, ALU.add)\
                        .then_inc(s_st, 1)

                def norm(ch):
                    dve.wait_ge(s_pow, ch + 1)
                    if not isinstance(ch, int):
                        dve.wait_ge(s_tr, ch * KD)
                    for s in range(SUB):
                        dve.tensor_scalar(xn[:, s, :], x[:, s, :], mv[:, s, 0:1], rstd[:, s:s + 1],
                                          ALU.subtract, ALU.mult).then_inc(s_xn, 1)

                dve.wait_ge(s_wt, 9 * 16)
                spread_of(0)
                dve.tensor_scalar(bdt1[:, :], bdt[:, :], 1e-3, None, ALU.add).then_inc(s_b1, 1)
                norm(0)
                for j, stage in enumerate((v, lg)):
                    dve.wait_ge(s_hi, j + 1)
                    dve.tensor_tensor(w_lo[:, 2 * j:2 * j + 2, :].rearrange("p k n -> p (k n)"),
                                      stage[:, :, :].rearrange("p m t -> p (m t)"),
                                      w_hi[:, 2 * j:2 * j + 2, :].rearrange("p k n -> p (k n)").bitcast(F32),
                                      ALU.subtract).then_inc(s_lo, 1)
                dve.wait_ge(s_b1, 1)
                dve.wait_ge(s_lo, 2)
                with dve.Fori(0, BATCH) as b:
                    dve.memset(xz[:, :, 0:HALO], 0.0).then_inc(s_halo, 1)
                    with dve.Fori(0, NCH) as k:
                        ch = b * NCH + k
                        dve.wait_ge(s_halo, ch + b + 1)
                        for m in range(MD):
                            dve.wait_ge(s_xe, ch * MD + m + 1)
                            if m >= 2:
                                dve.wait_ge(s_xs, ch * MD + m - 1)
                            acc = conv[:, m % 2, :]
                            dve.tensor_scalar(acc, xz[:, m, 0:CH], taps[:, m, 0:1], cbias[:, m:m + 1],
                                              ALU.mult, ALU.add).then_inc(s_cv, 1)
                            for j in range(1, TAPS):
                                dve.wait_ge(s_cv, ch * 32 + 4 * m + j)
                                dve.scalar_tensor_tensor(acc, xz[:, m, j:j + CH], taps[:, m, j:j + 1], acc,
                                                         ALU.mult, ALU.add).then_inc(s_cv, 1)
                            if m == 1:
                                spread_of(ch + 1)
                            if m == 3:
                                norm(ch + 1)
                        dve.tensor_copy(xz[:, :, 0:HALO], xz[:, :, CH:CH + HALO]).then_inc(s_halo, 1)
                        dve.wait_ge(s_xpm, ch + 1)
                        dve.wait_ge(s_xpo, ch * 16 + 1)
                        dve.tensor_copy(xp[:, :], ps_xp[0:NX, :]).then_inc(s_xpe, 1)
                        dve.wait_ge(s_xpe, ch + 1)
                        dve.tensor_reduce(bmax[:, :], xp[:, :], AX.X, ALU.max, apply_absolute_value=True).then_inc(s_in, 1)
                        dve.wait_ge(s_in, ch * 4 + 1)
                        dve.tensor_scalar(bdiag[:, :], ident[0:NX, 0:NX], bmax[:, 0:1], None, ALU.mult).then_inc(s_bd, 1)
                        dve.wait_ge(s_dt, ch * 2 + 1)
                        for m in range(MD):
                            dve.wait_ge(s_abs, ch * MD + m + 1)
                            dve.tensor_scalar(v[:, m, :], ps_r[:, m % RING, :], bdt1[:, m:m + 1], 1e-3, ALU.add, ALU.max)\
                                .then_inc(s_v, 1)
                        dve.wait_ge(s_xs, ch * MD + MD)
                        dve.tensor_reduce(xmax[:, :], xs[:, :, :], AX.X, ALU.max, apply_absolute_value=True)\
                            .then_inc(s_xm, 1)
                        dve.wait_ge(s_bb, ch + 1)
                        dve.wait_ge(s_xm, ch + 2)
                        dve.tensor_tensor(umax[:, :, :], bcast(xmax[:, :], [(1, MD), (0, NS)]),
                                          bcast(ps_b[:, 1:1 + NS], [(0, MD), (1, NS)]), ALU.mult).then_inc(s_in, 1)
                        dve.wait_ge(s_in, ch * 4 + 2)
                        dve.tensor_tensor(inside[:, :, :], umax[:, :, :], margin[:, :, :], ALU.is_le).then_inc(s_in, 1)
                        dve.wait_ge(s_in, ch * 4 + 3)
                        dve.tensor_tensor(within[:, :, :], within[:, :, :], inside[:, :, :], ALU.min).then_inc(s_in, 1)
                        dve.wait_ge(s_in, ch * 4 + 4)
                dve.tensor_reduce(inside1[:, :], within[:, :, :], AX.XY, ALU.min).then_inc(s_fl, 1)
                dve.wait_ge(s_fl, 2)
                dve.tensor_scalar(clips[:, :], ps_b[0:1, 0:1], P - 0.5, None, ALU.is_lt).then_inc(s_fl, 1)
                dve.wait_ge(s_fl, 3)


def scan(nc, sb, sem, ident, mask_d, clips, xs_d, dt_d, zs_d, xp_d, w_d, y_d):
    STEPS = MD * NS
    CHUNKS = BATCH * NCH
    XB, GB, QB = 4, 4, 8
    LAG = 3
    ON_DVE = (1, 3)
    ADD_AT = {6: 1, 7: 3, 8: 5, 10: 7, 12: 9, 14: 11, NS: 13, NS + 2: 15}
    ND = len(ON_DVE) * NS // 4
    NP = NS - ND
    with ExitStack() as c:
        w = sb("w_s", [P, 2, W_COLS], c=c)
        xs, dt, zs = sb("xs_s", [P, XB, CH + 1], c=c), sb("dt_s", [P, 2, CH], c=c), sb("zs_s", [P, 2, CH], c=c)
        cc = sb("cc", [P, NS, CH], c=c)
        bt = sb("bt", [P, GRP, NX], c=c)
        dm = sb("dm", [P, GRP, NS, 32], c=c)
        dd = sb("dd", [P, NS, CH], c=c)
        xd = sb("xd", [P, GRP, 2, 2, 32], c=c)
        xt = sb("xt", [P, 2, GRP, P], c=c)
        g, q = sb("g", [P, GB, CH], c=c), sb("q", [P, QB, CH], c=c)
        carry = sb("carry", [P, MD, NS], c=c)
        y = sb("y", [P, 2, CH], c=c)
        part = sb("part", [P, 2, CH], c=c)
        xpd = sb("xpd", [NX, 2 * CH], c=c)
        b_r, c_r, bc = sb("b_r", [NS, CH], c=c), sb("c_r", [NS, CH], c=c), sb("bc", [NS, CH], c=c)
        b_ahead = sb("b_ahead", [P, NS], c=c)
        neg_u0 = sb("neg_u0", [P, NS], c=c)
        neg_u = sb("neg_u", [P, CH], c=c)
        fac, lim = sb("fac", [P, CH, 2], c=c), sb("lim", [P, CH, 2], c=c)
        ps_a = c.enter_context(nc.psum_tensor("ps_a", [P, 2, CH], F32))
        ps_d = c.enter_context(nc.psum_tensor("ps_d", [P, 2, 2, 8, 32], F32))
        ps_y = c.enter_context(nc.psum_tensor("ps_y", [P, 2, CH], F32))
        ps_x = c.enter_context(nc.psum_tensor("ps_x", [P, CH], F32))
        ps_m = c.enter_context(nc.psum_tensor("ps_m", [P, CH], F32))

        S = lambda n: sem("s_" + n, c)
        s_pass = S("pass")
        s_xpl, s_ba, s_btp, s_bt, s_dm, s_bc = S("xpl"), S("ba"), S("btp"), S("bt"), S("dm"), S("bc")
        s_slot, s_cc = [S("slot0"), S("slot1")], [S(f"cc{i}") for i in range(4)]
        s_xsl = [S(f"xsl{i}") for i in range(XB)]
        s_xd, s_tr, s_xt, s_dps, s_dd = S("xd"), S("tr"), S("xt"), S("dps"), S("dd")
        s_a, s_g, s_q, s_n, s_acc = S("a"), S("g"), S("q"), S("n"), S("acc")
        s_fin, s_half, s_bcm, s_car, s_slow = S("fin"), S("half"), S("bcm"), S("carry"), S("slow")
        s_yo = [S("yo0"), S("yo1")]
        C_FIN, C_Q, C_G, C_YO, C_ACC = XB, NS, 2, 1, 1
        ACC = ND + 1

        def x_loads(ch, m):
            return ch * (16 * MD // XB) + 16 * (m // XB) + 16

        def slot_loads(ch, m):
            return ch * (48 * MD // 2) + 48 * (m // 2) + 48

        def pe_states(s):
            return sum(1 for i in range(s) if i % 4 not in ON_DVE)

        def acc_steps(s):
            return (s // NS) * ACC + 1 + sum(1 for i in range(s - s % NS, s + 1) if i % 4 in ON_DVE)

        with nc.Block() as block:
            @block.sync
            def _(sp):
                def load_tile(b, k, m):
                    e = m % 2
                    sp.dma_start(dt[:, e, :], dt_d[b, m, :, bass.ts(k, CH)]).then_inc(s_slot[e], 16)
                    sp.dma_start(w[:, e, :], w_d[m, :, :]).then_inc(s_slot[e], 16)
                    sp.dma_start(zs[:, e, :], zs_d[b, m, :, bass.ts(k, CH)]).then_inc(s_slot[e], 16)

                def load_c(b, k, i):
                    row = xp_d[b, 1 + NS + 4 * i:5 + NS + 4 * i, bass.ds(k * CH + 1, CH)]
                    sp.dma_start(cc[:, 4 * i:4 * i + 4, :], row.partition_broadcast(P)).then_inc(s_cc[i], 16)

                def load_projection(b, k):
                    for early in range(2):
                        sp.dma_start(xpd[:, :].rearrange("p (b s j) -> p b s j", s=2, j=32)[:, :, early, :],
                                     xp_d[b, :, bass.ds(k * CH + early, CH)].rearrange("p (b j) -> p b j", j=32))\
                            .then_inc(s_xpl, 16)
                    sp.dma_start(b_r[:, :], xp_d[b, 1:1 + NS, bass.ds(k * CH + 1, CH)]).then_inc(s_xpl, 16)
                    sp.dma_start(c_r[:, :], xp_d[b, 1 + NS:NX, bass.ds(k * CH + 1, CH)]).then_inc(s_xpl, 16)

                def load_b_ahead(b, k):
                    row = xp_d[b, 1:1 + NS, bass.ds(k * CH, 1)].rearrange("n o -> (n o)")
                    sp.dma_start(b_ahead[:, :], row.partition_broadcast(P),
                                 allow_slow_non_contiguous=True).then_inc(s_ba, 16)

                load_projection(0, 0)
                load_tile(0, 0, 0)
                for i in range(4):
                    load_c(0, 0, i)
                load_b_ahead(0, 0)
                with sp.Fori(0, BATCH) as b:
                    with sp.Fori(0, NCH) as k:
                        ch = b * NCH + k
                        after = (ch + 1) % CHUNKS
                        b1, k1 = after // NCH, after % NCH
                        for m in range(MD):
                            sp.wait_ge(s_fin, ch * MD + m + C_FIN)
                            if m + 1 < MD:
                                load_tile(b, k, m + 1)
                            else:
                                load_tile(b1, k1, 0)
                            if m > 0:
                                sp.dma_start(y_d[b, m - 1, :, bass.ts(k, CH)], y[:, (m - 1) % 2, :])\
                                    .then_inc(s_yo[(m - 1) % 2], 16)
                            if m == 0:
                                sp.wait_ge(s_dm, ch * 2 + 2)
                                sp.sem_inc(s_pass, 1)
                                sp.wait_ge(s_bc, ch + 1)
                                sp.sem_inc(s_pass, 1)
                                load_projection(b1, k1)
                        for i in range(4):
                            sp.sem_inc(s_pass, 1)
                            sp.wait_ge(s_q, ch * STEPS + STEPS - NS + 4 * i + 4 + C_Q)
                            load_c(b1, k1, i)
                        sp.wait_ge(s_fin, ch * MD + MD + C_FIN)
                        sp.dma_start(y_d[b, MD - 1, :, bass.ts(k, CH)], y[:, (MD - 1) % 2, :])\
                            .then_inc(s_yo[(MD - 1) % 2], 16)
                        load_b_ahead(b1, k1)
                for e in range(2):
                    sp.wait_ge(s_yo[e], CHUNKS * 16 * MD // 2 + C_YO)
                sp.wait_ge(s_slot[0], CHUNKS * 48 * MD // 2 + 48)
                sp.wait_ge(s_ba, CHUNKS * 16 + 16)
                for i in range(4):
                    sp.wait_ge(s_cc[i], CHUNKS * 16 + 16)

            @block.gpsimd
            def _(pool):
                pool.sem_inc(s_fin, C_FIN)
                pool.sem_inc(s_q, C_Q)
                pool.sem_inc(s_g, C_G)
                pool.sem_inc(s_acc, C_ACC)
                for e in range(2):
                    pool.sem_inc(s_yo[e], C_YO)
                with pool.Fori(0, CHUNKS) as ch:
                    for s in range(STEPS):
                        n = s % NS
                        if s < NS and n % 4 == 0:
                            pool.wait_ge(s_cc[n // 4], ch * 16 + 16)
                        pool.wait_ge(s_g, ch * STEPS + s + 1 + C_G)
                        if s >= QB:
                            r = s - QB
                            if r % 4 in ON_DVE:
                                pool.wait_ge(s_acc, ch * (MD * ACC) + acc_steps(r) + C_ACC)
                            else:
                                pool.wait_ge(s_n, ch * (MD * NP) + pe_states(r + 1))
                        pool.tensor_tensor(q[:, s % QB, :], g[:, s % GB, :], cc[:, n, :], ALU.mult).then_inc(s_q, 1)

            @block.scalar
            def _(act):
                def load_x(ch, b, k, m):
                    act.wait_ge(s_fin, ch * MD + m + 1 - XB + C_FIN)
                    act.dma_start(xs[:, m % XB, :], xs_d[b, m % MD, :, bass.ds(k * CH, CH + 1)])\
                        .then_inc(s_xsl[m % XB], 16)

                def double_x(ch, m):
                    act.wait_ge(s_xsl[m % XB], x_loads(ch, m))
                    act.activation(xd[:, :, :, :, :].rearrange("p g b s j -> p (g b) s j"),
                                   bcast(xs[:, m % XB, 0:1], [(32, 2 * GRP), (1, 2), (1, 32)]), ACT.Copy)\
                        .then_inc(s_xd, 1)

                def turned(ch, m, p):
                    act.wait_ge(s_tr, ch * (2 * MD) + 2 * m + p + 1)
                    act.activation(xt[:, m % 2, 4 * p:4 * p + 4, :], ps_x[:, :], ACT.Copy).then_inc(s_xt, 1)

                def keep_bt(ch):
                    act.wait_ge(s_btp, ch + 1)
                    act.activation(bt[:, :, :], ps_x[:, 0:GRP * NX], ACT.Copy).then_inc(s_bt, 1)

                def move_d(ch, half, i):
                    if i == 0 and half >= 1:
                        act.wait_ge(s_g, ch * STEPS + 8 * (half - 1) + C_G)
                    act.wait_ge(s_dps, ch * STEPS + 8 * half + i + 1)
                    n0, t0 = 8 * (half % 2), 128 * (i // 2) + 32 * (i % 2)
                    act.activation(bcast(dd[:, n0, t0:t0 + 1], [(64, 2), (CH, 8), (1, 32)]),
                                   ps_d[:, i % 2, :, :, :], ACT.Copy).then_inc(s_dd, 1)

                load_x(0, 0, 0, 0)
                load_x(0, 0, 0, 1)
                keep_bt(0)
                double_x(0, 0)
                for p in range(2):
                    turned(0, 0, p)
                for i in range(8):
                    move_d(0, 0, i)
                with act.Fori(0, BATCH) as b:
                    with act.Fori(0, NCH) as k:
                        ch = b * NCH + k
                        after = (ch + 1) % CHUNKS
                        for m in range(MD):
                            e = m % 2
                            act.wait_ge(s_slot[e], slot_loads(ch, m))
                            for n in range(NS):
                                s = m * NS + n
                                act.wait_ge(s_g, ch * STEPS + s - 1 + C_G)
                                act.activation(ps_a[:, n % 2, :], dt[:, e, :], ACT.Exp,
                                               scale=w[:, e, W_A + n:W_A + n + 1]).then_inc(s_a, 1)
                                if n == 0:
                                    double_x(ch, m + 1)
                                if n == 9:
                                    if m + 2 < MD:
                                        load_x(ch, b, k, m + 2)
                                    else:
                                        load_x(ch, after // NCH, after % NCH, m + 2)
                                if n in (3, 6):
                                    turned(ch, m + 1, n // 4)
                                if n == 10 and m == MD - 2:
                                    keep_bt(ch + 1)
                                move_d(ch, 2 * m + n // 8 + 1, n % 8)
                act.wait_ge(s_xsl[0], x_loads(CHUNKS, 0))
                act.wait_ge(s_xsl[1], x_loads(CHUNKS, 1))

            @block.tensor
            def _(pe):
                def turn(ch, m, p):
                    if p == 0:
                        pe.wait_ge(s_xd, ch * MD + m + 1)
                    if p == 0 and m % MD == 0:
                        pe.wait_ge(s_bt, ch + m // MD + 1)
                    if 2 * m + p > 0:
                        pe.wait_ge(s_xt, ch * (2 * MD) + 2 * m + p)
                    for i in range(4):
                        last = pe.transpose(ps_x[:, i * P:(i + 1) * P],
                                            xd[:, 4 * p + i, :, :, :].rearrange("p b s j -> p (b s j)"), ident[:, :])
                    last.then_inc(s_tr, 1)

                def turn_projection(ch):
                    pe.wait_ge(s_xpl, ch * 64 + 64)
                    pe.sem_inc(s_pass, 1)
                    for i in range(GRP):
                        last = pe.transpose(ps_x[:, i * NX:(i + 1) * NX], xpd[:, i * P:(i + 1) * P],
                                            ident[0:NX, 0:NX])
                    last.then_inc(s_btp, 1)

                def make_d(ch, half, i):
                    m, n0 = half // 2, 8 * (half % 2)
                    if half > 0 or i >= 2:
                        pe.wait_ge(s_dd, ch * STEPS + 8 * half + i - 1)
                    if half % 2 == 0:
                        pe.wait_ge(s_xt, ch * (2 * MD) + 2 * m + i // 4 + 1)
                    if i == 0 and half % (2 * MD) < 2:
                        pe.wait_ge(s_dm, ch * 2 + 2 * (half // (2 * MD)) + half % 2 + 1)
                    rows = slice(64 * (i % 2), 64 * (i % 2) + 64)
                    for j in range(2):
                        grp = 2 * (i // 2) + j
                        last = pe.matmul(ps_d[:, i % 2, j, :, :], xt[rows, m % 2, grp, :],
                                         dm[rows, grp, n0:n0 + 8, :], start=True, stop=True)
                    last.then_inc(s_dps, 1)

                def weigh_bc(ch, m):
                    pe.wait_ge(s_bc, ch + 1)
                    pe.wait_ge(s_acc, ch * (MD * ACC) + m * ACC + C_ACC)
                    pe.wait_ge(s_slot[m % 2], slot_loads(ch, m))
                    pe.matmul(ps_m[:, :], w[0:NS, m % 2, W_INVT:W_INVT + P], bc[:, :], start=True, stop=True)\
                        .then_inc(s_bcm, 1)

                def sum_state(ch, s):
                    m, n = s // NS, s % NS
                    if n % 4 in ON_DVE:
                        return
                    if n == 0 and m >= 2:
                        pe.wait_ge(s_fin, ch * MD + m - 1 + C_FIN)
                    pe.wait_ge(s_q, ch * STEPS + s + 1 + C_Q)
                    pe.matmul(ps_y[:, m % 2, :], w[:, m % 2, n * P:(n + 1) * P], q[:, s % QB, :],
                              start=(n == 0), stop=(pe_states(n + 1) == NP)).then_inc(s_n, 1)

                turn_projection(0)
                turn(0, 0, 0)
                turn(0, 0, 1)
                for i in range(8):
                    make_d(0, 0, i)
                with pe.Fori(0, CHUNKS) as ch:
                    for m in range(MD):
                        for n in range(NS):
                            s = m * NS + n
                            make_d(ch, 2 * m + n // 8 + 1, n % 8)
                            if n in (1, 4):
                                turn(ch, m + 1, n // 4)
                            if n == 8 and m == MD - 2:
                                pe.wait_ge(s_xt, ch * (2 * MD) + 2 * m + 4)
                                turn_projection(ch + 1)
                            if s >= LAG:
                                sum_state(ch, s - LAG)
                            if n == 3:
                                weigh_bc(ch, m)
                    for s in range(STEPS - LAG, STEPS):
                        sum_state(ch, s)

            @block.vector
            def _(dve):
                def make_dm(ch, h):
                    dve.wait_ge(s_bt, ch + 1)
                    dve.tensor_tensor(dm[:, :, 8 * h:8 * h + 8, :], bcast(mask_d[:, 0:1], [(0, GRP), (0, 8), (1, 32)]),
                                      bcast(bt[:, 0, 8 * h + 1:8 * h + 2], [(NX, GRP), (1, 8), (0, 32)]),
                                      ALU.mult).then_inc(s_dm, 1)

                def make_bc(ch):
                    dve.wait_ge(s_xpl, ch * 64 + 64)
                    dve.tensor_tensor(bc[:, :], b_r[:, :], c_r[:, :], ALU.mult).then_inc(s_bc, 1)

                must_clip = dve.value_load(clips[0:1, 0:1], min_val=0, max_val=1)
                dve.memset(fac[:, :, 1], -1.0).then_inc(s_slow, 1)
                for h in range(2):
                    make_dm(0, h)
                make_bc(0)
                with dve.Fori(0, BATCH) as b:
                    dve.memset(carry[:, :, :], 0.0).then_inc(s_car, 1)
                    with dve.Fori(0, NCH) as k:
                        ch = b * NCH + k

                        def start_sum(m):
                            dve.wait_ge(s_bcm, ch * MD + m + 1)
                            dve.wait_ge(s_xsl[m % XB], x_loads(ch, m))
                            dve.wait_ge(s_slot[m % 2], slot_loads(ch, m))
                            dve.scalar_tensor_tensor(ps_m[:, :], ps_m[:, :], w[:, m % 2, W_D:W_D + 1],
                                                     xs[:, m % XB, 1:CH + 1], ALU.add, ALU.mult).then_inc(s_acc, 1)

                        def add_state(s):
                            m, n = s // NS, s % NS
                            dve.wait_ge(s_acc, ch * (MD * ACC) + acc_steps(s) - 1 + C_ACC)
                            dve.wait_ge(s_q, ch * STEPS + s + 1 + C_Q)
                            dst = part[:, m % 2, :] if acc_steps(s) == (m + 1) * ACC else ps_m[:, :]
                            dve.scalar_tensor_tensor(dst, q[:, s % QB, :], w[:, m % 2, W_INV + n:W_INV + n + 1],
                                                     ps_m[:, :], ALU.mult, ALU.add).then_inc(s_acc, 1)

                        def finish(m):
                            dve.wait_ge(s_n, ch * (MD * NP) + NP * (m + 1))
                            dve.wait_ge(s_acc, ch * (MD * ACC) + ACC * (m + 1) + C_ACC)
                            dve.wait_ge(s_yo[m % 2], ch * (16 * MD // 2) + 16 * (m // 2) + C_YO)
                            dve.tensor_tensor(y[:, m % 2, :], ps_y[:, m % 2, :], part[:, m % 2, :], ALU.add)\
                                .then_inc(s_half, 1)
                            dve.wait_ge(s_half, ch * MD + m + 1)
                            dve.tensor_tensor(y[:, m % 2, :], y[:, m % 2, :], zs[:, m % 2, :], ALU.mult).then_inc(s_fin, 1)

                        def keep(m, n, slot):
                            dve.tensor_copy(carry[:, m, bass.ds(n, 4)], g[:, slot:slot + 4, CH - 1]).then_inc(s_car, 1)

                        def clipped_step(m, n, i, s):
                            at = s * 7 + ch * MD + m + 2

                            def link(ins, j):
                                ins.then_inc(s_slow, 1)
                                dve.wait_ge(s_slow, at + j + 1)
                            free = g[:, i, :]
                            a, d = ps_a[:, i % 2, :], dd[:, bass.ds(n, 1), :].rearrange("p o t -> p (o t)")
                            lim_n = w[:, m % 2, bass.ds(W_LIM + n, 1)]
                            link(dve.tensor_tensor_scan(neg_u[:, :], d, d, neg_u0[:, bass.ds(n, 1)], ALU.add, ALU.bypass), 0)
                            link(dve.tensor_tensor_scan(free, d, a, carry[:, m, bass.ds(n, 1)], ALU.add, ALU.mult), 1)
                            link(dve.tensor_tensor(neg_u[:, :], free, neg_u[:, :], ALU.subtract), 2)
                            dve.tensor_scalar(lim[:, :, 0], neg_u[:, :], -1.0, lim_n, ALU.mult, ALU.add).then_inc(s_slow, 1)
                            dve.tensor_scalar(lim[:, :, 1], neg_u[:, :], lim_n, None, ALU.add).then_inc(s_slow, 1)
                            link(dve.tensor_scalar(fac[:, :, 0], a, -1.0, None, ALU.mult), 5)
                            link(dve.tensor_tensor_scan(lim[:, :, :].rearrange("p t o -> p (t o)"),
                                                        fac[:, :, :].rearrange("p t o -> p (t o)"),
                                                        lim[:, :, :].rearrange("p t o -> p (t o)"),
                                                        0.0, ALU.mult, ALU.min), 6)
                            dve.tensor_tensor(g[:, i, :], free, lim[:, :, 1], ALU.subtract).then_inc(s_g, 1)

                        dve.wait_ge(s_car, ch * (STEPS // 4) + b + 1)
                        dve.sem_inc(s_pass, 1)
                        for m in range(MD):
                            if m == MD - 1:
                                dve.wait_ge(s_dps, ch * STEPS + 16 * m + 8)
                                make_dm(ch + 1, 0)
                            with dve.If(must_clip > 0):
                                if m == 0:
                                    dve.wait_ge(s_ba, ch * 16 + 16)
                                dve.wait_ge(s_xsl[m % XB], x_loads(ch, m))
                                dve.wait_ge(s_slot[m % 2], slot_loads(ch, m))
                                dve.tensor_scalar(neg_u0[:, :], b_ahead[:, :], xs[:, m % XB, 0:1], -1.0, ALU.mult, ALU.mult)\
                                    .then_inc(s_slow, 1)
                                for h in range(2):
                                    dve.wait_ge(s_dd, ch * STEPS + 8 * (2 * m + h + 1))
                                    dve.sem_inc(s_pass, 1)
                                    with dve.Fori(0, 2) as j:
                                        for i in range(4):
                                            n = j * 4 + (8 * h + i)
                                            s = ch * STEPS + m * NS + n
                                            dve.wait_ge(s_slow, s * 7 + ch * MD + m + 2)
                                            dve.wait_ge(s_a, s + 1)
                                            dve.wait_ge(s_q, s + 1 - GB + C_Q)
                                            clipped_step(m, n, i, s + 0)
                                        dve.wait_ge(s_g, ch * STEPS + m * NS + j * 4 + 8 * h + 4 + C_G)
                                        dve.sem_inc(s_pass, 1)
                                        keep(m, j * 4 + 8 * h, 0)
                                    if h == 0:
                                        start_sum(m)
                                    for n in range(8 * h, 8 * h + 8):
                                        if n % 4 in ON_DVE:
                                            add_state(m * NS + n)
                                    if h == 0 and m > 0:
                                        finish(m - 1)
                                    if h == 0 and m == MD - 1:
                                        dve.wait_ge(s_dps, ch * STEPS + STEPS)
                                        make_dm(ch + 1, 1)
                                        dve.wait_ge(s_bcm, ch * MD + MD)
                                        make_bc(ch + 1)
                            with dve.Else():
                                for n in range(NS):
                                    s = m * NS + n
                                    if n % 8 == 0:
                                        dve.wait_ge(s_dd, ch * STEPS + s + 8)
                                    dve.wait_ge(s_a, ch * STEPS + s + 1)
                                    if n % 4 == 0 and s > 0:
                                        dve.wait_ge(s_car, ch * (STEPS // 4) + b + 1 + s // 4)
                                    if s >= GB:
                                        dve.wait_ge(s_q, ch * STEPS + s - GB + 1 + C_Q)
                                    dve.tensor_tensor_scan(g[:, s % GB, :], dd[:, n, :], ps_a[:, n % 2, :],
                                                           carry[:, m, n:n + 1], ALU.add, ALU.mult).then_inc(s_g, 1)
                                    if n == 4:
                                        start_sum(m)
                                    if n == 5 and m > 0:
                                        finish(m - 1)
                                    if n in ADD_AT and ADD_AT[n] % 4 in ON_DVE:
                                        add_state(m * NS + ADD_AT[n])
                                    if m > 0 and n + NS in ADD_AT and ADD_AT[n + NS] % 4 in ON_DVE:
                                        add_state((m - 1) * NS + ADD_AT[n + NS])
                                    if n == 9 and m == MD - 1:
                                        dve.wait_ge(s_dps, ch * STEPS + STEPS)
                                        make_dm(ch + 1, 1)
                                        dve.wait_ge(s_bcm, ch * MD + MD)
                                        make_bc(ch + 1)
                                    if n % 4 == 3:
                                        dve.wait_ge(s_g, ch * STEPS + s + 1 + C_G)
                                        keep(m, n - 3, 0)
                                if m == MD - 1:
                                    for at in (NS, NS + 1, NS + 2):
                                        if at in ADD_AT and ADD_AT[at] % 4 in ON_DVE:
                                            add_state(m * NS + ADD_AT[at])
                        finish(MD - 1)


def ffn(nc, sb, sem, t_in, ident, minus_half, y_d, out):
    CHUNKS = BATCH * NCH
    RING = 4
    with ExitStack() as c:
        wo_hi, wo_lo = sb("wo_hi", [P, MD, DM], F32R, c), sb("wo_lo", [P, MD, DM], F32R, c)
        ws_hi, ws_lo = sb("ws_hi", [P, KD, DM], F32R, c), sb("ws_lo", [P, KD, DM], F32R, c)
        we_hi, we_lo = sb("we_hi", [P, KD, DM], F32R, c), sb("we_lo", [P, KD, DM], F32R, c)
        wg = sb("wg", [P, KD, P], c=c)
        wg_hi, wg_lo = sb("wg_hi", [P, KD, P], F32R, c), sb("wg_lo", [P, KD, P], F32R, c)
        gt = sb("gt", [8, CH], c=c)
        bias = sb("bias", [P, DM], c=c)
        y_hi = sb("y_hi", [P, MD, CH], F32R, c)
        y_lo = sb("y_lo", [P, 2, MD, CH], F32R, c)
        x = sb("x_c", [P, 2, SUB, DM], c=c)
        stats, mv = sb("stats_c", [P, SUB, 6], c=c), sb("mv_c", [P, SUB, 2], c=c)
        var, rstd = sb("var_c", [P, SUB], c=c), sb("rstd_c", [P, SUB], c=c)
        xn = sb("xn_c", [P, SUB, DM], c=c)
        t_hi, t_lo = sb("t_hi", [P, SUB, KD, P], F32R, c), sb("t_lo", [P, SUB, KD, P], F32R, c)
        xb = sb("xb_c", [P, SUB, DM], c=c)
        o = sb("o_c", [P, 2, SUB, DM], c=c)
        gmax, gate = sb("gmax", [P, SUB], c=c), sb("gate", [P, SUB, 8], c=c)
        z, rz = sb("z", [P, SUB], c=c), sb("rz", [P, SUB], c=c)
        top = sb("top", [P, SUB, 8], c=c)
        den, rden = sb("den", [P, SUB], c=c), sb("rden", [P, SUB], c=c)
        pick, wsum = sb("pick", [P, SUB, TOPK], c=c), sb("wsum", [P, SUB], c=c)
        ps_t = c.enter_context(nc.psum_tensor("ps_t_c", [P, 2, DM], F32))
        ps = c.enter_context(nc.psum_tensor("ps_c", [P, RING, DM], F32))
        ps_g = c.enter_context(nc.psum_tensor("ps_g", [P, DM], F32))
        S = lambda n: sem("c_" + n, c)
        s_pass = S("pass")
        s_wt, s_hi, s_lo, s_yh, s_yl = S("weights"), S("hi"), S("lo"), S("yh"), S("yl")
        s_st, s_pow, s_xn, s_xb, s_o, s_x1 = S("stats"), S("pow"), S("xn"), S("xb"), S("o"), S("x1")
        s_x, s_y, s_out = [S("lx0"), S("lx1")], [S("ly0"), S("ly1")], [S("out0"), S("out1")]
        s_one, s_tr, s_te, s_tl, s_g, s_s, s_e = S("one"), S("tr"), S("te"), S("tl"), S("g"), S("s"), S("e")
        s_gm, s_gt = S("gm"), S("gt")
        s_gx, s_ge, s_w, s_sx, s_fin = S("gx"), S("ge"), S("w"), S("sx"), S("fin")
        ITER = CHUNKS // 2
        LN_STEPS = 2 * SUB
        DV = LN_STEPS + 9
        C_SX = C_FIN = SUB

        parts = ((o[:, :, :, :].rearrange("p e s d -> p (e s) d"), wo_hi, wo_lo),
                 (x[:, 0, :, :], ws_hi, ws_lo), (x[:, 1, :, :], we_hi, we_lo), (wg[:, :, :], wg_hi, wg_lo))

        def rows(tensor, ch):
            return tensor[bass.ts(ch, CH), :].rearrange("(s p) d -> p s d", p=P)

        with nc.Block() as block:
            @block.sync
            def _(sp):
                def load_y(ch, e):
                    sp.dma_start(y_lo[:, e, :, :].bitcast(F32), y_d[ch // NCH, :, :, bass.ts(ch % NCH, CH)]
                                 .rearrange("m p t -> p m t")).then_inc(s_y[e], 16)

                def load_x(ch, e):
                    sp.dma_start(x[:, e, :, :], rows(t_in["x"], ch)).then_inc(s_x[e], 16)

                for name, dst in (("W_outT", parts[0][0]), ("W_sharedT", parts[1][0]), ("W_expertT", parts[2][0])):
                    sp.dma_start(dst, t_in[name].rearrange("(k p) n -> p k n", p=P)).then_inc(s_wt, 16)
                sp.wait_ge(s_ge, 2)
                sp.dma_start(wg[:, :, 0:GATES], t_in["W_gate"].rearrange("(k p) n -> p k n", p=P)).then_inc(s_wt, 16)
                sp.dma_start(bias[:, :], t_in["bias"].partition_broadcast(P)).then_inc(s_wt, 16)
                for e in range(2):
                    load_y(e, e)
                sp.wait_ge(s_lo, len(parts))
                for e in range(2):
                    load_x(e, e)
                with sp.Fori(0, ITER) as it:
                    for e in range(2):
                        ch = it * 2 + e
                        after = (it * 2 + (e + 2)) % CHUNKS
                        sp.wait_ge(s_o, ch * SUB + SUB)
                        sp.sem_inc(s_pass, 1)
                        load_y(after, e)
                        sp.wait_ge(s_xn, ch * SUB + SUB)
                        sp.sem_inc(s_pass, 1)
                        sp.wait_ge(s_xb, ch * SUB + SUB)
                        load_x(after, e)
                for e in range(2):
                    sp.wait_ge(s_x[e], ITER * 16 + 16)
                    sp.wait_ge(s_y[e], ITER * 16 + 16)

            @block.gpsimd
            def _(pool):
                pool.sem_inc(s_fin, C_FIN)
                pool.sem_inc(s_sx, C_SX)
                for e in range(2):
                    pool.sem_inc(s_out[e], 1)
                pool.memset(gate[:, :, :], -1.0).then_inc(s_ge, 1)
                pool.memset(wg[:, :, :], 0.0).then_inc(s_ge, 1)

                def inverse_spread(n):
                    pool.wait_ge(s_st, n)
                    pool.tensor_tensor(rstd[:, :], var[:, :], minus_half[:, :], ALU.pow).then_inc(s_pow, 1)

                def rest_of_y(ch, e, count):
                    pool.wait_ge(s_yh, ch + 1)
                    pool.wait_ge(s_y[e], count)
                    pool.tensor_tensor(y_lo[:, e, :, :], y_lo[:, e, :, :].bitcast(F32), y_hi[:, :, :].bitcast(F32),
                                       ALU.subtract).then_inc(s_yl, 1)

                rest_of_y(0, 0, 16)
                inverse_spread(1)
                rest_of_y(1, 1, 16)
                with pool.Fori(0, ITER) as it:
                    for e in range(2):
                        ch = it * 2 + e
                        for i in range(SUB):
                            pool.wait_ge(s_fin, ch * SUB + (i + 1 - SUB + C_FIN))
                            pool.tensor_tensor(xb[:, i, :], x[:, e, i, :], bias[:, :], ALU.add).then_inc(s_xb, 1)
                        inverse_spread(ch + 2)
                        rest_of_y(ch + 2, e, it * 16 + 32)

            @block.scalar
            def _(act):
                def upper_y(ch, e, count):
                    act.wait_ge(s_y[e], count)
                    act.activation(y_hi[:, :, :], y_lo[:, e, :, :].bitcast(F32), ACT.Copy).then_inc(s_yh, 1)

                act.wait_ge(s_wt, 5 * 16)
                for whole, hi, lo in parts:
                    act.activation(hi[:, :, :], whole, ACT.Copy).then_inc(s_hi, 1)
                upper_y(0, 0, 16)
                act.wait_ge(s_o, SUB)
                upper_y(1, 1, 16)
                with act.Fori(0, ITER) as it:
                    for e in range(2):
                        ch = it * 2 + e
                        for i in range(SUB):
                            act.wait_ge(s_tr, ch * SUB + i + 1)
                            act.activation(t_hi[:, i, :, :], ps_t[:, i % 2, :], ACT.Copy).then_inc(s_te, 1)
                        act.wait_ge(s_gm, ch + 1)
                        act.activation(gt[:, :], ps_g[0:8, :], ACT.Copy).then_inc(s_gt, 1)
                        act.wait_ge(s_gx, ch + 1)
                        act.activation(gate[:, :, 0:GATES], gate[:, :, 0:GATES], ACT.Exp).then_inc(s_ge, 1)
                        act.wait_ge(s_o, ch * SUB + 2 * SUB)
                        upper_y(ch + 2, e, it * 16 + 32)
                        act.wait_ge(s_fin, ch * SUB + SUB + C_FIN)
                        act.dma_start(rows(out, ch), o[:, e, :, :]).then_inc(s_out[e], 16)
                for e in range(2):
                    act.wait_ge(s_out[e], ITER * 16 + 1)

            @block.tensor
            def _(pe):
                def product(dst, a_hi, a_lo, b_hi, b_lo, tiles):
                    for j in range(tiles):
                        for p, (a, b) in enumerate(((a_hi, b_hi), (a_hi, b_lo), (a_lo, b_hi))):
                            last = pe.matmul(dst, a(j), b(j), start=(j + p == 0), stop=(j == tiles - 1 and p == 2))
                    return last

                def turn_gates(ch):
                    pe.wait_ge(s_gt, ch + 1)
                    pe.sem_inc(s_pass, 1)
                    for i in range(SUB):
                        last = pe.transpose(ps_g[:, 8 * i:8 * i + 8], gt[:, i * P:(i + 1) * P], ident[0:8, 0:8])
                    last.then_inc(s_g, 1)

                def project(ch, e, waits, between=None):
                    pe.wait_ge(s_yl, ch + 1)
                    for i in range(SUB):
                        if waits is not None:
                            s, n = waits[i]
                            pe.wait_ge(s, n)
                        at = slice(i * P, (i + 1) * P)
                        product(ps[:, i, :], lambda m: y_hi[:, m, at], lambda m: y_lo[:, e, m, at],
                                lambda m: wo_hi[:, m, :], lambda m: wo_lo[:, m, :], MD).then_inc(s_o, 1)
                        if i == 0 and between is not None:
                            between()

                pe.wait_ge(s_lo, len(parts))
                project(0, 0, None)
                with pe.Fori(0, ITER) as it:
                    for e in range(2):
                        ch = it * 2 + e
                        for i in range(SUB):
                            pe.wait_ge(s_xn, ch * SUB + i + 1)
                            if i >= 2:
                                pe.wait_ge(s_tl, ch * SUB + i - 1)
                            for q in range(KD):
                                last = pe.transpose(ps_t[:, i % 2, q * P:(q + 1) * P], xn[:, i, q * P:(q + 1) * P],
                                                    ident[:, :])
                            last.then_inc(s_tr, 1)

                        def times(i, dst, b_hi, b_lo):
                            return product(dst, lambda k: t_hi[:, i, k, :], lambda k: t_lo[:, i, k, :],
                                           lambda k: b_hi[:, k, :], lambda k: b_lo[:, k, :], KD)
                        pe.wait_ge(s_tl, ch * SUB + SUB)
                        product(ps_g[:, :], lambda k: wg_hi[:, k, :], lambda k: wg_lo[:, k, :],
                                lambda k: t_hi[:, :, k, :], lambda k: t_lo[:, :, k, :], KD).then_inc(s_gm, 1)
                        project(ch + 1, 1 - e, [(s_sx, ch * SUB + 3 - SUB + C_SX), (s_fin, ch * SUB + 3 - SUB + C_FIN),
                                                (s_sx, ch * SUB + 4 - SUB + C_SX), (s_fin, ch * SUB + 4 - SUB + C_FIN)],
                                lambda: turn_gates(ch))
                        for i in range(SUB):
                            for j, (b_hi, b_lo, own, done) in enumerate(((ws_hi, ws_lo, s_sx, s_s), (we_hi, we_lo, s_fin, s_e))):
                                bank = (2 * i + j) % RING
                                if i < 2:
                                    pe.wait_ge(s_x1, ch * SUB + SUB + bank + 1)
                                else:
                                    pe.wait_ge(own, ch * SUB + i - 1 + C_FIN)
                                times(i, ps[:, bank, :], b_hi, b_lo).then_inc(done, 1)

            @block.vector
            def _(dve):
                at = [0]

                def step(ins, base, wait=True):
                    at[0] += 1
                    ins.then_inc(s_one, 1)
                    if wait:
                        dve.wait_ge(s_one, base + at[0])
                        dve.sem_inc(s_pass, 1)

                def residual_and_norm(ch, e, loads, base):
                    dve.wait_ge(s_x[e], loads)
                    for i in range(SUB):
                        dve.wait_ge(s_o, ch * SUB + i + 1)
                        dve.tensor_tensor(x[:, e, i, :], ps[:, i, :], x[:, e, i, :], ALU.add).then_inc(s_x1, 1)
                    for i in range(SUB):
                        dve.wait_ge(s_x1, ch * SUB + i + 1)
                        step(dve.bn_stats(stats[:, i, :], x[:, e, i, :]), base, i == SUB - 1)
                    for i in range(SUB):
                        step(dve.bn_aggr(mv[:, i, :], stats[:, i, :]), base, i == SUB - 1)
                    dve.tensor_scalar(var[:, :], mv[:, :, 1], EPS, None, ALU.add).then_inc(s_st, 1)
                    dve.wait_ge(s_pow, ch + 1)
                    for i in range(SUB):
                        dve.tensor_scalar(xn[:, i, :], x[:, e, i, :], mv[:, i, 0:1], rstd[:, i:i + 1],
                                          ALU.subtract, ALU.mult).then_inc(s_xn, 1)

                for j, (whole, hi, lo) in enumerate(parts):
                    dve.wait_ge(s_hi, j + 1)
                    dve.tensor_tensor(lo[:, :, :], whole, hi[:, :, :].bitcast(F32), ALU.subtract).then_inc(s_lo, 1)
                residual_and_norm(0, 0, 16, 0)
                with dve.Fori(0, ITER) as it:
                    for e in range(2):
                        ch = it * 2 + e
                        at[0], base = 0, ch * DV + LN_STEPS
                        for i in range(SUB):
                            dve.wait_ge(s_te, ch * SUB + i + 1)
                            dve.tensor_tensor(t_lo[:, i, :, :], ps_t[:, i % 2, :].rearrange("p (k t) -> p k t", t=P),
                                              t_hi[:, i, :, :].bitcast(F32), ALU.subtract).then_inc(s_tl, 1)
                        dve.wait_ge(s_g, ch + 1)
                        logits = bcast(ps_g[:, 0:1], [(8, SUB), (1, GATES)])
                        step(dve.tensor_reduce(gmax[:, :], logits, AX.X, ALU.max), base)
                        dve.tensor_tensor(gate[:, :, 0:GATES], logits, bcast(gmax[:, 0:1], [(1, SUB), (0, GATES)]),
                                          ALU.subtract).then_inc(s_gx, 1)
                        dve.wait_ge(s_ge, ch + 3)
                        step(dve.tensor_reduce(z[:, :], gate[:, :, 0:GATES], AX.X, ALU.add), base)
                        step(dve.reciprocal(rz[:, :], z[:, :]), base)
                        step(dve.tensor_tensor(gate[:, :, 0:GATES], gate[:, :, 0:GATES],
                                               bcast(rz[:, 0:1], [(1, SUB), (0, GATES)]), ALU.mult), base)
                        for i in range(SUB):
                            last = dve.max(top[:, i, :], gate[:, i, :])
                        step(last, base)
                        step(dve.tensor_reduce(den[:, :], top[:, :, 0:TOPK], AX.X, ALU.add), base)
                        step(dve.reciprocal(rden[:, :], den[:, :]), base)
                        step(dve.tensor_tensor(pick[:, :, :], top[:, :, 0:TOPK],
                                               bcast(rden[:, 0:1], [(1, SUB), (0, TOPK)]), ALU.mult), base)
                        step(dve.tensor_reduce(wsum[:, :], pick[:, :, :], AX.X, ALU.add), base)
                        residual_and_norm(ch + 1, 1 - e, it * 16 + (16 + 16 * e), base)
                        assert at[0] == DV
                        dve.wait_ge(s_out[e], it * 16 + 1)
                        for i in range(SUB):
                            dve.wait_ge(s_xb, ch * SUB + i + 1)
                            dve.wait_ge(s_s, ch * SUB + i + 1)
                            dve.tensor_tensor(xb[:, i, :], ps[:, (2 * i) % RING, :], xb[:, i, :], ALU.add)\
                                .then_inc(s_sx, 1)
                            dve.wait_ge(s_sx, ch * SUB + i + 1 + C_SX)
                            dve.wait_ge(s_e, ch * SUB + i + 1)
                            dve.scalar_tensor_tensor(o[:, e, i, :], ps[:, (2 * i + 1) % RING, :], wsum[:, i:i + 1],
                                                     xb[:, i, :], ALU.mult, ALU.add).then_inc(s_fin, 1)


def kernel(**inputs):
    import numpy as np
    import concourse.bacc as bacc
    from concourse.bass_utils import run_bass_kernel_spmd

    a = {k[3:].split("_", 1)[1]: np.asarray(v) for k, v in inputs.items()}
    def columns(v):
        return v.reshape(-1, P).T

    laid = {
        "x": a["x"].reshape(TOKENS, DM), "ln_gamma": columns(a["ln_gamma"]), "ln_beta": columns(a["ln_beta"]),
        "W_inT": a["W_in"].T, "conv_w": a["conv_w"].reshape(DI, TAPS), "conv_b": columns(a["conv_b"]),
        "A_log": a["A_log"], "D_param": columns(a["D_param"]), "W_xprojT": a["W_xproj"].T, "W_dtT": a["W_dt"].T,
        "b_dt": columns(a["b_dt"]), "W_outT": a["W_out"].T, "W_sharedT": a["W_shared"].T, "W_expertT": a["W_expert"].T,
        "W_gate": a["W_gate"], "bias": a["bias"],
    }
    nc = bacc.Bacc("TRN2", target_bir_lowering=False, num_devices=1)
    arrays, t_in = {}, {}
    for name, v in laid.items():
        arrays["in_" + name] = np.ascontiguousarray(v)
        t_in[name] = nc.dram_tensor("in_" + name, v.shape, mybir.dt.from_np(v.dtype), kind="ExternalInput").ap()
    out = nc.dram_tensor("out", (TOKENS, DM), F32, kind="ExternalOutput").ap()
    build(nc, t_in, out)
    r = run_bass_kernel_spmd(nc, [arrays], core_ids=[0])
    return r.results[0]["out"].reshape(BATCH, LEN, DM)
```
